# Optimizing a Trainium2 kernel written in Bass

```python
import numpy as np
import jax
import jax.numpy as jnp

def _softmax(x, axis=-1):
    return jax.nn.softmax(x, axis=axis)

def _gelu(x):
    return jax.nn.gelu(x, approximate=True)

def _silu(x):
    return jax.nn.silu(x)

def _sigmoid(x):
    return jax.nn.sigmoid(x)

def _layernorm(x, axis=-1, eps=1e-05):
    m = jnp.mean(x, axis=axis, keepdims=True)
    v = jnp.var(x, axis=axis, keepdims=True)
    return (x - m) / jnp.sqrt(v + eps)

def _scatter_add(tgt, idx, src, axis=0):
    return tgt.at[idx].add(src)

def _segment_sum(src, seg, n):
    return jax.ops.segment_sum(src, seg, n)
kernel_name = 'mk_pixart_seq_d2_seqx_r4_282118'

def setup_inputs(seed: int=0):
    np.random.seed(seed)
    _w = jnp.asarray

    def _rec_inputs():
        import jax
        import jax.numpy as jnp
        _rk = jax.random.key(seed)
        x = -0.0003929 + 0.9999 * jax.random.normal(jax.random.fold_in(_rk, 1), (16, 256, 256), jnp.float32)
        _lenS = 256 - jax.random.randint(jax.random.fold_in(_rk, 7), (16,), 0, max(1, 256 // 4) + 1, jnp.int32)
        _lenS2 = 256 - jax.random.randint(jax.random.fold_in(_rk, 8), (16,), 0, max(1, 256 // 4) + 1, jnp.int32)
        cond_1024 = 0.00782532 + 1.00527 * jax.random.normal(jax.random.fold_in(_rk, 11), (16, 256), jnp.float32)
        _ctx_1024P = jax.random.normal(jax.random.fold_in(_rk, 12), (16, 16, 256), jnp.float32)
        _ctx_1024c = jax.random.dirichlet(jax.random.fold_in(_rk, 512), 0.3 * jnp.ones((16,), jnp.float32), (16, 256))
        _ctx_1024t = jnp.einsum('bsk,bkd->bsd', _ctx_1024c, _ctx_1024P)
        _ctx_1024t = _ctx_1024t * jax.lax.rsqrt(jnp.mean(jnp.square(_ctx_1024t)) + 1e-12) * 0.953939
        ctx_1024 = -0.000761806 + 0.999296 * (_ctx_1024t + 0.3 * jax.random.normal(jax.random.fold_in(_rk, 612), (16, 256, 256), jnp.float32))
        return (x, cond_1024, ctx_1024)
    x, cond_1024, ctx_1024 = _rec_inputs()

    def _L0_xcond_setup():
        import jax, jax.numpy as jnp
        import numpy as np
        H = 256
        RH = 2 * H
        E = 3
        B, T, P = (8, 512, 64)
        LN_EPS = 1e-05

        def _layer_norm(x, gamma, beta):
            mu = jnp.mean(x, axis=-1, keepdims=True)
            var = jnp.mean(jnp.square(x - mu), axis=-1, keepdims=True)
            return (x - mu) * jax.lax.rsqrt(var + LN_EPS) * gamma + beta
        key = jax.random.key(seed)
        ks = jax.random.split(key, 24)
        s = lambda fan_in: 1.0 / np.sqrt(fan_in)
        inp = {'mix_hidden_states': jax.random.normal(ks[0], (B, T, H), jnp.float32), 'global_anchor': jax.random.normal(ks[1], (B, H), jnp.float32), 'prototype_bank': jax.random.normal(ks[2], (B, P, H), jnp.float32), 'ln_gamma': jnp.ones((H,), jnp.float32), 'ln_beta': jnp.zeros((H,), jnp.float32), 'Wq': jax.random.normal(ks[3], (H, H), jnp.float32) * s(H), 'Wk': jax.random.normal(ks[4], (H, H), jnp.float32) * s(H), 'Wv': jax.random.normal(ks[5], (H, H), jnp.float32) * s(H), 'router_W': jax.random.normal(ks[6], (3 * H, E), jnp.float32) * s(3 * H), 'router_b': jnp.zeros((E,), jnp.float32), 'e_w1': jax.random.normal(ks[7], (E, 3 * H, RH), jnp.float32) * s(3 * H), 'e_b1': jnp.zeros((E, RH), jnp.float32), 'e_w2': jax.random.normal(ks[8], (E, RH, H), jnp.float32) * s(RH), 'e_b2': jnp.zeros((E, H), jnp.float32), 'gate_w1': jax.random.normal(ks[9], (3 * H, H), jnp.float32) * s(3 * H), 'gate_b1': jnp.zeros((H,), jnp.float32), 'gate_w2': jax.random.normal(ks[10], (H, H), jnp.float32) * s(H), 'gate_b2': jnp.zeros((H,), jnp.float32), 'out_w': jax.random.normal(ks[11], (H, H), jnp.float32) * s(H), 'out_b': jnp.zeros((H,), jnp.float32)}
        return inp
    _L0_xcond_all = _L0_xcond_setup()
    _L0_xcond_in = {k: v for k, v in _L0_xcond_all.items() if k in ('ln_gamma', 'ln_beta', 'Wq', 'Wk', 'Wv', 'router_W', 'router_b', 'e_w1', 'e_b1', 'e_w2', 'e_b2', 'gate_w1', 'gate_b1', 'gate_w2', 'gate_b2', 'out_w', 'out_b')}
    del _L0_xcond_all

    def _L1_xcond_setup():
        import jax, jax.numpy as jnp
        import numpy as np
        C = 256
        H = 16
        D = C // H
        WIN = 128
        SHIFT = 64
        TOPK = 16
        HID = 1024
        EPS = 1e-06

        def _ln(x):
            x32 = x.astype(jnp.float32)
            m = x32.mean(-1, keepdims=True)
            v = jnp.mean((x32 - m) ** 2, axis=-1, keepdims=True)
            return ((x32 - m) * jax.lax.rsqrt(v + EPS)).astype(x.dtype)

        def _self_attn(h, w_qkv, b_qkv, w_so, b_so):
            B, L, _ = h.shape
            qkv = h @ w_qkv + b_qkv
            qkv = jnp.roll(qkv, -SHIFT, axis=1)
            nw = L // WIN
            qkv = qkv.reshape(B, nw, WIN, 3, H, D)
            q, k, v = (qkv[:, :, :, 0], qkv[:, :, :, 1], qkv[:, :, :, 2])
            scores = jnp.einsum('bnqhd,bnkhd->bnhqk', q, k) / jnp.sqrt(jnp.float32(D)).astype(h.dtype)
            attn = jax.nn.softmax(scores, axis=-1)
            o = jnp.einsum('bnhqk,bnkhd->bnqhd', attn, v).reshape(B, L, C)
            o = jnp.roll(o, SHIFT, axis=1)
            return o @ w_so + b_so

        def _topk_cross_attn(h, ctx, w_q, b_q, w_kv, b_kv, w_co, b_co):
            B, L, _ = h.shape
            Lc = ctx.shape[1]
            q = (h @ w_q + b_q).reshape(B, L, H, D)
            kv = (ctx @ w_kv + b_kv).reshape(B, Lc, 2, H, D)
            k, v = (kv[:, :, 0], kv[:, :, 1])
            scores = jnp.einsum('bqhd,bkhd->bhqk', q, k) / jnp.sqrt(jnp.float32(D)).astype(h.dtype)
            top_s, top_i = jax.lax.top_k(scores, TOPK)
            attn = jax.nn.softmax(top_s, axis=-1)
            v_bh = jnp.transpose(v, (0, 2, 1, 3))
            vg = jnp.take_along_axis(v_bh[:, :, None, :, :], top_i[..., None], axis=3)
            o = jnp.einsum('bhqk,bhqkd->bqhd', attn, vg).reshape(B, L, C)
            return o @ w_co + b_co

        def _swiglu(h, w_m1, b_m1, w_m2, b_m2):
            u = h @ w_m1 + b_m1
            a, b = (u[..., :HID], u[..., HID:])
            return jax.nn.silu(a) * b @ w_m2 + b_m2
        key = jax.random.key(seed)
        ks = jax.random.split(key, 24)
        s = 0.02
        inp = {'x': jax.random.normal(ks[0], (2, 1024, C), jnp.float32), 'mod': jax.random.normal(ks[1], (2, C), jnp.float32), 'context': jax.random.normal(ks[2], (2, 256, C), jnp.float32), 'w_ada': jax.random.normal(ks[3], (C, 9 * C), jnp.float32) * s, 'b_ada': jnp.zeros((9 * C,), jnp.float32), 'w_qkv': jax.random.normal(ks[4], (C, 3 * C), jnp.float32) * s, 'b_qkv': jnp.zeros((3 * C,), jnp.float32), 'w_so': jax.random.normal(ks[5], (C, C), jnp.float32) * s, 'b_so': jnp.zeros((C,), jnp.float32), 'w_q': jax.random.normal(ks[6], (C, C), jnp.float32) * s, 'b_q': jnp.zeros((C,), jnp.float32), 'w_kv': jax.random.normal(ks[7], (C, 2 * C), jnp.float32) * s, 'b_kv': jnp.zeros((2 * C,), jnp.float32), 'w_co': jax.random.normal(ks[8], (C, C), jnp.float32) * s, 'b_co': jnp.zeros((C,), jnp.float32), 'w_m1': jax.random.normal(ks[9], (C, 2 * HID), jnp.float32) * s, 'b_m1': jnp.zeros((2 * HID,), jnp.float32), 'w_m2': jax.random.normal(ks[10], (HID, C), jnp.float32) * s, 'b_m2': jnp.zeros((C,), jnp.float32)}
        return inp
    _L1_xcond_all = _L1_xcond_setup()
    _L1_xcond_in = {k: v for k, v in _L1_xcond_all.items() if k in ('w_ada', 'b_ada', 'w_qkv', 'b_qkv', 'w_so', 'b_so', 'w_q', 'b_q', 'w_kv', 'b_kv', 'w_co', 'b_co', 'w_m1', 'b_m1', 'w_m2', 'b_m2')}
    del _L1_xcond_all
    return {'x': x, 'cond_1024': cond_1024, 'ctx_1024': ctx_1024, 'L0_xcond_ln_gamma': _L0_xcond_in['ln_gamma'], 'L0_xcond_ln_beta': _L0_xcond_in['ln_beta'], 'L0_xcond_Wq': _L0_xcond_in['Wq'], 'L0_xcond_Wk': _L0_xcond_in['Wk'], 'L0_xcond_Wv': _L0_xcond_in['Wv'], 'L0_xcond_router_W': _L0_xcond_in['router_W'], 'L0_xcond_router_b': _L0_xcond_in['router_b'], 'L0_xcond_e_w1': _L0_xcond_in['e_w1'], 'L0_xcond_e_b1': _L0_xcond_in['e_b1'], 'L0_xcond_e_w2': _L0_xcond_in['e_w2'], 'L0_xcond_e_b2': _L0_xcond_in['e_b2'], 'L0_xcond_gate_w1': _L0_xcond_in['gate_w1'], 'L0_xcond_gate_b1': _L0_xcond_in['gate_b1'], 'L0_xcond_gate_w2': _L0_xcond_in['gate_w2'], 'L0_xcond_gate_b2': _L0_xcond_in['gate_b2'], 'L0_xcond_out_w': _L0_xcond_in['out_w'], 'L0_xcond_out_b': _L0_xcond_in['out_b'], 'L1_xcond_w_ada': _L1_xcond_in['w_ada'], 'L1_xcond_b_ada': _L1_xcond_in['b_ada'], 'L1_xcond_w_qkv': _L1_xcond_in['w_qkv'], 'L1_xcond_b_qkv': _L1_xcond_in['b_qkv'], 'L1_xcond_w_so': _L1_xcond_in['w_so'], 'L1_xcond_b_so': _L1_xcond_in['b_so'], 'L1_xcond_w_q': _L1_xcond_in['w_q'], 'L1_xcond_b_q': _L1_xcond_in['b_q'], 'L1_xcond_w_kv': _L1_xcond_in['w_kv'], 'L1_xcond_b_kv': _L1_xcond_in['b_kv'], 'L1_xcond_w_co': _L1_xcond_in['w_co'], 'L1_xcond_b_co': _L1_xcond_in['b_co'], 'L1_xcond_w_m1': _L1_xcond_in['w_m1'], 'L1_xcond_b_m1': _L1_xcond_in['b_m1'], 'L1_xcond_w_m2': _L1_xcond_in['w_m2'], 'L1_xcond_b_m2': _L1_xcond_in['b_m2']}

def reference(x, cond_1024, ctx_1024, L0_xcond_ln_gamma, L0_xcond_ln_beta, L0_xcond_Wq, L0_xcond_Wk, L0_xcond_Wv, L0_xcond_router_W, L0_xcond_router_b, L0_xcond_e_w1, L0_xcond_e_b1, L0_xcond_e_w2, L0_xcond_e_b2, L0_xcond_gate_w1, L0_xcond_gate_b1, L0_xcond_gate_w2, L0_xcond_gate_b2, L0_xcond_out_w, L0_xcond_out_b, L1_xcond_w_ada, L1_xcond_b_ada, L1_xcond_w_qkv, L1_xcond_b_qkv, L1_xcond_w_so, L1_xcond_b_so, L1_xcond_w_q, L1_xcond_b_q, L1_xcond_w_kv, L1_xcond_b_kv, L1_xcond_w_co, L1_xcond_b_co, L1_xcond_w_m1, L1_xcond_b_m1, L1_xcond_w_m2, L1_xcond_b_m2):
    import jax
    import jax.numpy as jnp

    def _L0_xcond_ref(mix_hidden_states, global_anchor, prototype_bank, ln_gamma, ln_beta, Wq, Wk, Wv, router_W, router_b, e_w1, e_b1, e_w2, e_b2, gate_w1, gate_b1, gate_w2, gate_b2, out_w, out_b):
        import jax, jax.numpy as jnp
        import numpy as np
        H = 256
        RH = 2 * H
        E = 3
        B, T, P = (8, 512, 64)
        LN_EPS = 1e-05

        def _layer_norm(x, gamma, beta):
            mu = jnp.mean(x, axis=-1, keepdims=True)
            var = jnp.mean(jnp.square(x - mu), axis=-1, keepdims=True)
            return (x - mu) * jax.lax.rsqrt(var + LN_EPS) * gamma + beta
        x = mix_hidden_states
        nx = _layer_norm(x, ln_gamma, ln_beta)
        q = nx @ Wq
        k = prototype_bank @ Wk
        v = prototype_bank @ Wv
        scores = jnp.einsum('bth,bph->btp', q, k) * H ** (-0.5)
        weights = jax.nn.softmax(scores, axis=-1)
        evidence = jnp.einsum('btp,bph->bth', weights, v)
        anchor = jnp.broadcast_to(global_anchor[:, None, :], nx.shape)
        combined = jnp.concatenate([nx, evidence, anchor], axis=-1)
        router_logits = combined @ router_W + router_b
        router_probs = jax.nn.softmax(router_logits, axis=-1)
        h = jax.nn.silu(jnp.einsum('btc,ecr->bter', combined, e_w1) + e_b1)
        expert_out = jnp.einsum('bter,erh->bteh', h, e_w2) + e_b2
        routed = jnp.sum(expert_out * router_probs[..., None], axis=-2)
        g = jax.nn.sigmoid(jax.nn.silu(combined @ gate_w1 + gate_b1) @ gate_w2 + gate_b2)
        refined_delta = g * (routed @ out_w + out_b)
        return x + refined_delta

    def _L1_xcond_ref(x, mod, context, w_ada, b_ada, w_qkv, b_qkv, w_so, b_so, w_q, b_q, w_kv, b_kv, w_co, b_co, w_m1, b_m1, w_m2, b_m2):
        import jax, jax.numpy as jnp
        import numpy as np
        C = 256
        H = 16
        D = C // H
        WIN = 128
        SHIFT = 64
        TOPK = 16
        HID = 1024
        EPS = 1e-06

        def _ln(x):
            x32 = x.astype(jnp.float32)
            m = x32.mean(-1, keepdims=True)
            v = jnp.mean((x32 - m) ** 2, axis=-1, keepdims=True)
            return ((x32 - m) * jax.lax.rsqrt(v + EPS)).astype(x.dtype)

        def _self_attn(h, w_qkv, b_qkv, w_so, b_so):
            B, L, _ = h.shape
            qkv = h @ w_qkv + b_qkv
            qkv = jnp.roll(qkv, -SHIFT, axis=1)
            nw = L // WIN
            qkv = qkv.reshape(B, nw, WIN, 3, H, D)
            q, k, v = (qkv[:, :, :, 0], qkv[:, :, :, 1], qkv[:, :, :, 2])
            scores = jnp.einsum('bnqhd,bnkhd->bnhqk', q, k) / jnp.sqrt(jnp.float32(D)).astype(h.dtype)
            attn = jax.nn.softmax(scores, axis=-1)
            o = jnp.einsum('bnhqk,bnkhd->bnqhd', attn, v).reshape(B, L, C)
            o = jnp.roll(o, SHIFT, axis=1)
            return o @ w_so + b_so

        def _topk_cross_attn(h, ctx, w_q, b_q, w_kv, b_kv, w_co, b_co):
            B, L, _ = h.shape
            Lc = ctx.shape[1]
            q = (h @ w_q + b_q).reshape(B, L, H, D)
            kv = (ctx @ w_kv + b_kv).reshape(B, Lc, 2, H, D)
            k, v = (kv[:, :, 0], kv[:, :, 1])
            scores = jnp.einsum('bqhd,bkhd->bhqk', q, k) / jnp.sqrt(jnp.float32(D)).astype(h.dtype)
            top_s, top_i = jax.lax.top_k(scores, TOPK)
            attn = jax.nn.softmax(top_s, axis=-1)
            v_bh = jnp.transpose(v, (0, 2, 1, 3))
            vg = jnp.take_along_axis(v_bh[:, :, None, :, :], top_i[..., None], axis=3)
            o = jnp.einsum('bhqk,bhqkd->bqhd', attn, vg).reshape(B, L, C)
            return o @ w_co + b_co

        def _swiglu(h, w_m1, b_m1, w_m2, b_m2):
            u = h @ w_m1 + b_m1
            a, b = (u[..., :HID], u[..., HID:])
            return jax.nn.silu(a) * b @ w_m2 + b_m2
        m = jax.nn.silu(mod) @ w_ada + b_ada
        sh_msa, sc_msa, g_msa, sh_mca, sc_mca, g_mca, sh_mlp, sc_mlp, g_mlp = [m[:, i * C:(i + 1) * C][:, None, :] for i in range(9)]
        h = _ln(x) * (1 + sc_msa) + sh_msa
        h = _self_attn(h, w_qkv, b_qkv, w_so, b_so)
        x = x + h * g_msa
        h = _ln(x) * (1 + sc_mca) + sh_mca
        h = _topk_cross_attn(h, context, w_q, b_q, w_kv, b_kv, w_co, b_co)
        x = x + h * g_mca
        h = _ln(x) * (1 + sc_mlp) + sh_mlp
        h = _swiglu(h, w_m1, b_m1, w_m2, b_m2)
        x = x + h * g_mlp
        return x
    x = _L0_xcond_ref(x, cond_1024, ctx_1024, L0_xcond_ln_gamma, L0_xcond_ln_beta, L0_xcond_Wq, L0_xcond_Wk, L0_xcond_Wv, L0_xcond_router_W, L0_xcond_router_b, L0_xcond_e_w1, L0_xcond_e_b1, L0_xcond_e_w2, L0_xcond_e_b2, L0_xcond_gate_w1, L0_xcond_gate_b1, L0_xcond_gate_w2, L0_xcond_gate_b2, L0_xcond_out_w, L0_xcond_out_b)
    x = _L1_xcond_ref(x, cond_1024, ctx_1024, L1_xcond_w_ada, L1_xcond_b_ada, L1_xcond_w_qkv, L1_xcond_b_qkv, L1_xcond_w_so, L1_xcond_b_so, L1_xcond_w_q, L1_xcond_b_q, L1_xcond_w_kv, L1_xcond_b_kv, L1_xcond_w_co, L1_xcond_b_co, L1_xcond_w_m1, L1_xcond_b_m1, L1_xcond_w_m2, L1_xcond_b_m2)
    return x

_drawn_inputs = setup_inputs


def setup_inputs(seed=0):
    import zlib

    import numpy as np

    out = dict(_drawn_inputs(seed))
    spreads = {'L0_xcond_ln_gamma': (1.0, 0.2),
     'L0_xcond_ln_beta': (0.0, 0.621),
     'L0_xcond_router_b': (0.0, 0.8),
     'L0_xcond_e_b1': (0.0, 0.399),
     'L0_xcond_e_b2': (0.0, 0.1),
     'L0_xcond_gate_b1': (0.0, 0.8),
     'L0_xcond_gate_b2': (0.0, 0.8),
     'L0_xcond_out_b': (0.0, 0.1),
     'L1_xcond_b_ada': (0.0, 0.435),
     'L1_xcond_b_qkv': (0.0, 0.8),
     'L1_xcond_b_so': (0.0, 0.397),
     'L1_xcond_b_q': (0.0, 0.8),
     'L1_xcond_b_kv': (0.0, 0.8),
     'L1_xcond_b_co': (0.0, 0.385),
     'L1_xcond_b_m1': (0.0, 0.8),
     'L1_xcond_b_m2': (0.0, 1.615)}
    factors = {'L1_xcond_w_qkv': 8.0,
     'L1_xcond_w_so': 6.365,
     'L1_xcond_w_q': 5.194,
     'L1_xcond_w_kv': 3.492,
     'L1_xcond_w_co': 3.255,
     'L1_xcond_w_m1': 6.312,
     'L1_xcond_w_m2': 6.289}
    for name, (base, spread) in spreads.items():
        noise = np.random.default_rng([zlib.crc32(name.encode()), seed]).standard_normal(out[name].shape)
        drawn = base * np.exp(spread * noise) if base else spread * noise
        out[name] = jnp.asarray(drawn.astype(out[name].dtype))
    for name, factor in factors.items():
        out[name] = (out[name] * factor).astype(out[name].dtype)
    return out
```

```python
import concourse.bass as bass
from concourse import mybir
from contextlib import ExitStack

F32 = mybir.dt.float32
ALU = mybir.AluOpType
ACT = mybir.ActivationFunctionType
AX_X = mybir.AxisListType.X

P = 128
B, T, C = 16, 256, 256
NT, NC = T // P, C // P
E, RH = 3, 512
H, D = 16, 16
HPT = P // D
SHIFT = 64
WIN = 128
TOPK = 16
HID = 1024
EXP_COLS = E * RH
GATE_COL = EXP_COLS
ROUT_COL = GATE_COL + C
W1_COLS = ROUT_COL + E
NCH = (EXP_COLS + C) // P
EPS0, EPS1 = 1e-5, 1e-6
REPLACED = -3.0e38
VA = D + 1

SELF_GROUPS = 8
CROSS_GROUPS = 16
S_LAG, PV_LAG = 2, 3
FILL = {
    "start0": ["ctxT"], "start1": ["nxT", "kp"],
    ("self", 0): ["sc"], ("self", 3): ["PT"], ("self", 6): ["evT"], ("self", 8): ["lgT"],
    "heads1": ["lg", "h0"], "norm2": ["h1"],
    ("cross", 1): ["h2"], ("cross", 4): ["h3"], ("cross", 7): ["h4"], ("cross", 10): ["h5"],
    ("cross", 13): ["h6"], ("cross", 15): ["g"], ("cross", 17): ["y0"],
    "heads2": ["y1"], "norm3": ["y2"],
}


class Signal:

    def __init__(self, sem, per):
        self.sem, self.per = sem, per

    def at(self, b, n=None):
        return b * self.per + (self.per if n is None else n)


class Products:

    def __init__(self, plan, banks, written):
        self.banks, self.written = banks, written
        self.of, self.count = {}, [0] * len(banks)
        for name, k, raises in plan:
            self.of[name] = (k, self.count[k])
            self.count[k] += raises

    def bank(self, name):
        return self.banks[self.of[name][0]]

    def sem(self, name):
        return self.written[self.of[name][0]]

    def at(self, b, name, part=1):
        k, before = self.of[name]
        return b * self.count[k] + before + part


def later(b):
    return not (isinstance(b, int) and b == 0)


def build(nc, x, cond_1024, ctx_1024, ln_gamma, ln_beta, Wq, Wk, Wv, router_W, router_b, e_w1, e_b1, e_w2,
          e_b2, gate_w1, gate_b1, gate_w2, gate_b2, out_w, out_b, w_ada, b_ada, w_qkv, b_qkv, w_so, b_so,
          w_q, b_q, w_kv, b_kv, w_co, b_co, w_m1, b_m1, w_m2, b_m2, out):
    ctx = ExitStack()
    with ctx:
        def sb(name, shape, dt=F32):
            return ctx.enter_context(nc.sbuf_tensor(name, shape, dt))

        def sem(name):
            return ctx.enter_context(nc.semaphore(name))

        def signal(name, per):
            return Signal(sem(name), per)

        ident = sb("ident", [P, P])
        wqk = sb("wqk", [P, NC, C])
        w1 = sb("w1", [P, 2 * NC, W1_COLS])
        w2 = sb("w2", [P, EXP_COLS // P, C])
        wg2 = sb("wg2", [P, NC, C])
        wqkv = sb("wqkv", [P, NC, 3 * C])
        wso = sb("wso", [P, NC, C])
        wq2 = sb("wq2", [P, NC, C])
        wkv = sb("wkv", [P, NC, 2 * C])
        wco = sb("wco", [P, NC, C])
        wm1 = sb("wm1", [P, NC, 2 * HID])
        wm2 = sb("wm2", [P, HID // P, C])
        gamma = sb("gamma", [P, NC])
        beta = sb("beta", [P, NC])
        gate_b2_all = sb("gate_b2_all", [P, 1, C])
        out_b_all = sb("out_b_all", [P, C])
        e_b2_all = sb("e_b2_all", [P, E, C])
        bq1 = sb("bq1", [P, NC])
        bk1 = sb("bk1", [P, NC])
        bq2 = sb("bq2", [P, NC])
        bk2 = sb("bk2", [P, NC])
        bm1 = sb("bm1", [P, 2 * HID // P])
        bm1_half = sb("bm1_half", [P, HID // P])
        hid_bias = sb("hid_bias", [P, B, 2 * NCH])
        rout_bias = sb("rout_bias", [E, B])
        ada = sb("ada", [P, B, 6 * NC])
        head_mask = sb("head_mask", [P, HPT])

        minus_half = sb("minus_half", [P, NT, 1])

        x_in = sb("x_in", [P, NT, C])
        x_res = sb("x_res", [P, NT, C])
        ctx_in = sb("ctx_in", [P, NT, C])
        grow = sb("grow", [P, 6, C])

        WORK_COLS = 23400
        work = sb("work", [P, WORK_COLS])

        def carver():
            at = [0]

            def carve(*dims):
                n = 1
                for d in dims:
                    n *= d
                a, at[0] = at[0], at[0] + n
                assert at[0] <= WORK_COLS, at
                v = work[:, a:a + n]
                if len(dims) == 2:
                    v = v.rearrange("p (a b) -> p a b", a=dims[0])
                if len(dims) == 3:
                    v = v.rearrange("p (a b c) -> p a b c", a=dims[0], b=dims[1])
                return v
            return carve

        room = carver()
        ctxT = room(NC, T)
        nx = room(NT, C)
        p0 = nx
        nxT = room(NC, T)
        kpT = room(NC, T)
        pT0 = room(NT, T)
        evT = room(NC, T)
        th = room(2, 2, T)
        hid = room(NCH, T)
        zg = room(NT, C)
        acc = room(NT, C)
        x1 = room(NT, C)
        xn = room(NT, C)
        hT = room(NC, T)
        oT = hT
        qT = room(NC, T)
        kT1 = room(NC, T)
        kT2 = room(NC, T)
        KM = room(H, T)
        gated = KM[:, 0:HID // P, :]
        thm = KM[:, HID // P:HID // P + 4, :]
        va1 = room(NT, H, VA)
        va2 = room(NT, H, VA)
        es = room(3, 512)
        et = room(2, 512)
        s1 = room(512)
        s2 = room(2, 512)
        o = room(NT, C)
        xb = room(NT, C)
        tmp = room(NT, C)
        xs = room(NT, C)

        hb = sb("hb", [P, 2 * NCH])
        rb = sb("rb", [E, 1])
        ad = sb("ad", [P, 6 * NC])
        st0 = sb("st0", [P, NT, 6])
        mv0 = sb("mv0", [P, NT, 2])
        rstd0 = sb("rstd0", [P, NT, 1])
        st1 = sb("st1", [P, NT, 6])
        mv1 = sb("mv1", [P, NT, 2])
        rstd1 = sb("rstd1", [P, NT, 1])
        nm0 = sb("nm0", [P, NT])
        sum0 = sb("sum0", [P, NT])
        r0 = sb("r0", [P, NT])
        lgT = sb("lgT", [E, T])
        lmax = sb("lmax", [P, NT, 1])
        lsub = sb("lsub", [P, NT, E])
        lexp = sb("lexp", [P, NT, E])
        lsum = sb("lsum", [P, NT, 1])
        lrec = sb("lrec", [P, NT, 1])
        prob = sb("prob", [P, NT, E])
        nms = sb("nms", [P, 2, 4])
        m8 = sb("m8", [P, 2, 4, 8])
        nmc = sb("nmc", [P, 2, 2])
        ro = sb("ro", [P, NT, H, 1])

        weights_loaded = sem("weights_loaded")
        raw_loaded = sem("raw_loaded")
        pool_setup = sem("pool_setup")
        ident_ready = sem("ident_ready")
        cond_tanh_ready = sem("cond_tanh_ready")
        scond_ready = sem("scond_ready")
        setup_mm = sem("setup_mm")
        setup_ev = sem("setup_ev")
        rows_ready = sem("gate_rows_ready")
        rows_stored = sem("gate_rows_stored")
        setup_done = sem("setup_done")
        ones_ready = sem("ones_ready")
        x_loaded = signal("x_loaded", 48)
        ctx_loaded = signal("ctx_loaded", 16)
        grow_loaded = signal("gate_rows_loaded", 16)
        x_copied = signal("x_copied", 1)
        stored = signal("stored", 48)
        stats0 = signal("layer0_stats", 4)
        rstd0_ready = signal("layer0_rstd_ready", 2)
        nx_ready = signal("nx_ready", 2)
        hb_ready = signal("hidden_bias_ready", 1)
        rb_ready = signal("router_bias_ready", 1)
        ctxT_ready = signal("ctxT_ready", 1)
        nxT_ready = signal("nxT_ready", 2)
        kp_ready = signal("kp_ready", 1)
        nm0_ready = signal("layer0_max_ready", 1)
        exp0_ready = signal("layer0_exp_ready", 2)
        r0_ready = signal("layer0_recip_ready", 1)
        p0_ready = signal("layer0_weights_ready", 2)
        pT0_ready = signal("layer0_weightsT_ready", 1)
        evT_ready = signal("evT_ready", 1)
        lgT_ready = signal("logitsT_ready", 1)
        router = signal("router_vector", 5)
        lexp_ready = signal("router_exp_ready", 1)
        tanh0 = signal("layer0_tanh", NCH)
        plus0 = signal("layer0_tanh_plus_one", NCH // 2)
        hid_ready = signal("layer0_hidden_ready", NCH)
        mix = signal("experts_mixed", 12)
        zg_ready = signal("gate_sum_ready", 1)
        tg_ready = signal("gate_tanh_ready", 1)
        x1_ready = signal("x1_ready", 2)
        ad_ready = signal("ada_ready", 1)
        stats1 = signal("layer1_stats", 12)
        rstd1_ready = signal("layer1_rstd_ready", 6)
        xn_ready = signal("xn_ready", 6)
        hT_ready = signal("hT_ready", 6)
        q_ready = signal("q_ready", 4)
        k1_ready = signal("k1_ready", 2)
        k2_ready = signal("k2_ready", 2)
        va1_ready = signal("v1_ready", 2)
        va2_ready = signal("v2_ready", 2)
        km_ready = signal("masked_keys_ready", 2 * H)
        max1_ready = signal("self_max_ready", SELF_GROUPS)
        exp1_ready = signal("self_exp_ready", 4 * SELF_GROUPS)
        et1_ready = signal("self_weightsT_ready", SELF_GROUPS)
        top = signal("top16_vector", 9 * CROSS_GROUPS)
        exp2_ready = signal("cross_exp_ready", 2 * CROSS_GROUPS)
        sel_ready = signal("cross_selection_ready", CROSS_GROUPS)
        p2_ready = signal("cross_weights_ready", CROSS_GROUPS)
        et2_ready = signal("cross_weightsT_ready", CROSS_GROUPS)
        ro_ready = signal("heads_recip_ready", 4)
        o_ready = signal("heads_ready", 4)
        oT_ready = signal("headsT_ready", 2)
        xb_ready = signal("residual_plus_bias_ready", 3)
        gy_ready = signal("gated_out_ready", 3)
        xs_ready = signal("residual_ready", 3)
        tanh1 = signal("mlp_tanh", 8)
        plus1 = signal("mlp_tanh_plus_one", 8)
        mlp = signal("mlp_vector", 16)

        banks = [ctx.enter_context(nc.psum_tensor(f"bank{i}", [P, 512], F32)) for i in range(8)]
        written = [sem(f"bank{i}_written") for i in range(8)]
        L0 = Products([("ctxT", 0, 1), ("nxT", 1, 1), ("kp", 0, 1), ("sc", 1, 1), ("PT", 0, 1), ("evT", 1, 1),
                       ("lgT", 0, 1), ("lg", 1, 1)] + [(f"h{j}", j % 2, 1) for j in range(NCH // 2)]
                      + [("g", 1, 1)] + [(f"y{e}", e % 2, 1) for e in range(E)], banks[0:2], written[0:2])
        plan1 = [("k2", 0, 1), ("v2", 1, 1), ("hT1", 2, 1), ("q1", 0, 1), ("k1", 1, 1), ("v1", 3, 1)]
        for g in range(SELF_GROUPS):
            plan1 += [(("S1", g), g % 2, 1), (("T1", g), 2 + g % 2, 1)]
        plan1 += [(("O1", w), 4 + w, 4) for w in range(2)]
        plan1 += [("oT1", 2, 1), ("so", 3, 1), ("hT2", 2, 1), ("q2", 3, 1)]
        for g in range(CROSS_GROUPS):
            plan1 += [(("S2", g), g % 2, 1), (("T2", g), 2 + g % 2, 1)]
        plan1 += [(("O2", t), 4 + t, 8) for t in range(NT)]
        plan1 += [("oT2", 2, 1), ("co", 3, 1), ("hT3", 2, 1)]
        plan1 += [(("m", j), (0, 1, 3, 2)[j % 4], 1) for j in range(HID // P)]
        plan1 += [("y", 4, 1)]
        L1 = Products(plan1, banks[2:8], written[2:8])

        gate_rows = nc.dram_tensor("gate_rows", (B, 6, C), F32, kind="Internal").ap()

        raw = carver()
        raw_q, raw_k, raw_v, raw_o = [raw(NC, C) for _ in range(4)]
        tq, tk, tv = [raw(NC, C) for _ in range(3)]
        tw2 = raw(NC, EXP_COLS)
        raw_ev = raw(NC, W1_COLS)
        raw_an = raw(NC, W1_COLS)
        raw_ada = raw(NC, 9 * C)
        cond_col = raw(NC, B)
        cond_tanh = raw(NC, B)
        scond = raw(NC, B)
        hid_b = raw(NCH)
        ada_b = raw(6 * NC)
        rout_b = raw(1)
        eb2_col = raw(NC, E, 1)
        eb2_cols = raw(NC, E, P)
        bv_col = raw(NC, 2, 1)
        bv_cols = raw(NC, 2, B)
        gate_bias = raw(3, C)
        row_bias = raw(3, C)
        mrow = raw(6, C)

        def col(v):
            return v.rearrange("(c p) -> p c", p=P)

        def rows(v):
            return v.rearrange("(c p) n -> p c n", p=P)

        def row(v, n):
            return v.partition_broadcast(n)

        raw_loads = [
            (raw_q, rows(Wq)), (raw_k, rows(Wk)), (raw_v, rows(Wv)), (raw_o, rows(out_w)),
            (raw_ev[:, :, GATE_COL:ROUT_COL], rows(gate_w1[C:2 * C, :])),
            (raw_ev[:, :, ROUT_COL:W1_COLS], rows(router_W[C:2 * C, :])),
            (raw_an[:, :, GATE_COL:ROUT_COL], rows(gate_w1[2 * C:3 * C, :])),
            (raw_an[:, :, ROUT_COL:W1_COLS], rows(router_W[2 * C:3 * C, :])),
            (raw_ada, rows(w_ada)),
            (hid_b[:, 12:14], col(gate_b1)), (rout_b[0:E, :], router_b.rearrange("(e a) -> e a", a=1)),
        ]
        for e in range(E):
            raw_loads += [(w2[:, 4 * e:4 * e + 4, :], rows(e_w2[e])),
                          (raw_ev[:, :, e * RH:(e + 1) * RH], rows(e_w1[e, C:2 * C, :])),
                          (raw_an[:, :, e * RH:(e + 1) * RH], rows(e_w1[e, 2 * C:3 * C, :])),
                          (hid_b[:, 4 * e:4 * e + 4], col(e_b1[e])), (eb2_col[:, :, e, 0], col(e_b2[e])),
                          (ada_b[:, 4 * e:4 * e + 4], col(b_ada[3 * e * C:(3 * e + 2) * C])),
                          (gate_bias[0:B, e, :], row(b_ada[(3 * e + 2) * C:(3 * e + 3) * C], B))]
        raw_loads += [(row_bias[0:B, s, :], row(v, B)) for s, v in enumerate((b_so, b_co, b_m2))]
        raw_loads += [(bv_col[:, :, 0, 0], col(b_qkv[2 * C:3 * C])), (bv_col[:, :, 1, 0], col(b_kv[C:2 * C]))]
        raw_loads += [(cond_col[:, c, :], cond_1024[:, c * P:(c + 1) * P].rearrange("b p -> p b")) for c in range(NC)]
        weight_loads = [
            (w1[:, 0:NC, GATE_COL:ROUT_COL], rows(gate_w1[0:C, :])),
            (w1[:, 0:NC, ROUT_COL:W1_COLS], rows(router_W[0:C, :])),
            (wg2[:, :, :], rows(gate_w2)), (wqkv[:, :, :], rows(w_qkv)), (wso[:, :, :], rows(w_so)),
            (wq2[:, :, :], rows(w_q)), (wkv[:, :, :], rows(w_kv)), (wco[:, :, :], rows(w_co)),
            (wm1[:, :, :], rows(w_m1)), (wm2[:, :, :], rows(w_m2)),
            (gamma[:, :], col(ln_gamma)), (beta[:, :], col(ln_beta)),
            (gate_b2_all[:, 0, :], row(gate_b2, P)), (out_b_all[:, :], row(out_b, P)),
            (bq1[:, :], col(b_qkv[0:C])), (bk1[:, :], col(b_qkv[C:2 * C])),
            (bq2[:, :], col(b_q)), (bk2[:, :], col(b_kv[0:C])), (bm1[:, :], col(b_m1)),
        ] + [(w1[:, 0:NC, e * RH:(e + 1) * RH], rows(e_w1[e, 0:C, :])) for e in range(E)]
        RAW_LOADED, WEIGHTS_LOADED = 16 * len(raw_loads), 16 * len(weight_loads)

        SETUP = ([("tq", c) for c in range(NC)] + [("tk", c) for c in range(NC)] + [("tv", c) for c in range(NC)]
                 + [("tw2", k) for k in range(6)] + [("wqk", c) for c in range(NC)]
                 + [("ev", c, n) for c in range(NC) for n in range(0, W1_COLS, 512)]
                 + [("w2", k) for k in range(6)] + [("eb2", e) for e in range(E)]
                 + [("hid",), ("rout",), ("ada",)] + [("gate", s) for s in range(3)] + [("bias", s) for s in range(2)])

        block = ctx.enter_context(nc.Block())

        @block.sync
        def _(sp):
            with nc.allow_non_contiguous_dma(reason="vectors down the partitions, once"):
                for dst, src in raw_loads:
                    sp.dma_start(dst, src).then_inc(raw_loaded, 16)
                for dst, src in weight_loads:
                    sp.dma_start(dst, src).then_inc(weights_loaded, 16)

            def load_ctx(b):
                if later(b):
                    sp.wait_ge(L0.sem("evT"), L0.at(b - 1, "evT"))
                    sp.wait_ge(L0.sem("ctxT"), L0.at(b - 1, "ctxT"))
                sp.dma_start(ctx_in[:, :, :], ctx_1024[bass.ds(b, 1), :, :].rearrange("a (t p) c -> p (a t) c", p=P))\
                    .then_inc(ctx_loaded.sem, 16)

            def load_x(b):
                if later(b):
                    sp.wait_ge(x_copied.sem, x_copied.at(b - 1))
                    sp.wait_ge(nx_ready.sem, nx_ready.at(b - 1))
                for dst, lo in ((x_in[:, 0, :], SHIFT), (x_in[0:P - SHIFT, 1, :], SHIFT + P), (x_in[P - SHIFT:P, 1, :], 0)):
                    n = dst.shape[0]
                    sp.dma_start(dst, x[bass.ds(b, 1), lo:lo + n, :].rearrange("a p c -> (a p) c")).then_inc(x_loaded.sem, 16)

            def load_rows(b):
                if later(b):
                    sp.wait_ge(xb_ready.sem, xb_ready.at(b - 1))
                    sp.wait_ge(gy_ready.sem, gy_ready.at(b - 1))
                sp.dma_start(grow[:, :, :].rearrange("p s c -> p (s c)"),
                             gate_rows[bass.ds(b, 1), :, :].rearrange("a s c -> (a s c)").partition_broadcast(P))\
                    .then_inc(grow_loaded.sem, 16)

            def store(b):
                sp.wait_ge(xs_ready.sem, xs_ready.at(b))
                for src, lo in ((xs[:, 0, :], SHIFT), (xs[0:P - SHIFT, 1, :], SHIFT + P), (xs[P - SHIFT:P, 1, :], 0)):
                    n = src.shape[0]
                    sp.dma_start(out[bass.ds(b, 1), lo:lo + n, :].rearrange("a p c -> (a p) c"), src).then_inc(stored.sem, 16)

            load_x(0)
            load_ctx(0)
            sp.wait_ge(rows_ready, 1)
            sp.dma_start(gate_rows[:, :, :], mrow[0:B, :, :]).then_inc(rows_stored, 16)
            sp.wait_ge(rows_stored, 16)
            load_rows(0)
            load_x(1)
            load_ctx(1)
            with sp.Fori(1, B - 1) as i:
                store(i - 1)
                load_rows(i)
                load_x(i + 1)
                load_ctx(i + 1)
            store(B - 2)
            load_rows(B - 1)
            store(B - 1)
            sp.wait_ge(stored.sem, stored.at(B - 1))

        @block.gpsimd
        def _(pool):
            g = nc.gpsimd
            g.memset(ident[:, :], 0.0).then_inc(pool_setup, 1)
            pool.wait_ge(pool_setup, 1)
            g.affine_select(out=ident[:, :], in_=ident[:, :], compare_op=ALU.not_equal, fill=1.0,
                            base=0, pattern=[[-1, P]], channel_multiplier=1).then_inc(ident_ready, 1)
            g.memset(head_mask[:, :], 1.0).then_inc(pool_setup, 1)
            pool.wait_ge(pool_setup, 2)
            g.affine_select(out=head_mask[:, :], in_=head_mask[:, :], compare_op=ALU.is_ge, fill=0.0,
                            base=0, pattern=[[-D, HPT]], channel_multiplier=1).then_inc(pool_setup, 1)
            pool.wait_ge(pool_setup, 3)
            g.affine_select(out=head_mask[:, :], in_=head_mask[:, :], compare_op=ALU.is_ge, fill=0.0,
                            base=D - 1, pattern=[[D, HPT]], channel_multiplier=-1).then_inc(pool_setup, 1)
            pool.wait_ge(setup_done, 1)
            pool.wait_ge(rows_stored, 16)
            g.memset(va1[:, :, :, D:VA], 1.0).then_inc(ones_ready, 1)
            g.memset(va2[:, :, :, D:VA], 1.0).then_inc(ones_ready, 1)
            g.memset(minus_half[:, :, :], -0.5).then_inc(pool_setup, 1)
            pool.wait_ge(pool_setup, 5)

            def alone():
                pool.nop(nofuse=True)

            def fill(slot, a):
                for name in FILL.get(slot, []) if a is not None else []:
                    if name == "nxT":
                        pool.wait_ge(x_loaded.sem, x_loaded.at(a))
                        if later(a):
                            pool.wait_ge(x1_ready.sem, x1_ready.at(a - 1))
                        alone()
                        g.tensor_copy(x_res[:, :, :], x_in[:, :, :]).then_inc(x_copied.sem, 1)
                        inverse_deviation(a, stats0, 0, mv0, EPS0, rstd0, rstd0_ready)
                    if name == "sc":
                        pool.wait_ge(r0_ready.sem, r0_ready.at(a))
                        alone()
                        for t in range(NT):
                            g.tensor_scalar(p0[:, t, :], p0[:, t, :], r0[:, t:t + 1], None, ALU.mult)\
                                .then_inc(p0_ready.sem, 1)
                    if name[0] == "h":
                        j = int(name[1:])
                        pool.wait_ge(tanh0.sem, tanh0.at(a, 2 * j + 2))
                        alone()
                        g.tensor_scalar(th[:, j % 2, :, :], th[:, j % 2, :, :], 1.0, None, ALU.add)\
                            .then_inc(plus0.sem, 1)

            def masked_keys(src):
                for h in range(H):
                    g.tensor_scalar(KM[:, h, :], src[:, h // HPT, :], head_mask[:, h % HPT:h % HPT + 1], None, ALU.mult)\
                        .then_inc(km_ready.sem, 1)

            def inverse_deviation(b, stats, n, mv, eps, dst, ready):
                pool.wait_ge(stats.sem, stats.at(b, 4 * n + 4))
                alone()
                g.tensor_scalar(dst[:, :, :], mv[:, :, 1:2], eps, None, ALU.add).then_inc(ready.sem, 1)
                pool.wait_ge(ready.sem, ready.at(b, 2 * n + 1))
                g.tensor_tensor(dst[:, :, :], dst[:, :, :], minus_half[:, :, :], ALU.pow).then_inc(ready.sem, 1)

            def plus_bias(b, s, src):
                if s:
                    pool.wait_ge(xs_ready.sem, xs_ready.at(b, s))
                else:
                    pool.wait_ge(grow_loaded.sem, grow_loaded.at(b))
                    pool.wait_ge(x1_ready.sem, x1_ready.at(b))
                    if later(b):
                        pool.wait_ge(xs_ready.sem, xs_ready.at(b - 1))
                g.tensor_tensor(xb[:, :, :], src[:, :, :], grow[:, 2 * s + 1:2 * s + 2, :].broadcast_to([P, NT, C]), ALU.add)\
                    .then_inc(xb_ready.sem, 1)

            def iteration(a, b):
                if b is not None:
                    inverse_deviation(b, stats1, 0, mv1, EPS1, rstd1, rstd1_ready)
                    plus_bias(b, 0, x1)
                fill("start0", a)
                fill("start1", a)
                if b is not None:
                    pool.wait_ge(k1_ready.sem, k1_ready.at(b))
                    if later(b):
                        pool.wait_ge(gy_ready.sem, gy_ready.at(b - 1))
                    alone()
                    masked_keys(kT1)
                for s in range(SELF_GROUPS + PV_LAG):
                    fill(("self", s), a)
                if b is not None:
                    for s in (SELF_GROUPS - 2, SELF_GROUPS - 1):
                        pool.wait_ge(L1.sem(("S1", s)), L1.at(b, ("S1", s)))
                    pool.wait_ge(k2_ready.sem, k2_ready.at(b))
                    alone()
                    masked_keys(kT2)
                fill("heads1", a)
                if b is not None:
                    inverse_deviation(b, stats1, 1, mv1, EPS1, rstd1, rstd1_ready)
                    plus_bias(b, 1, xs)
                fill("norm2", a)
                for s in range(CROSS_GROUPS + PV_LAG):
                    if b is not None and s < CROSS_GROUPS:
                        pool.wait_ge(top.sem, top.at(b, 9 * s + 9))
                        alone()
                        g.tensor_scalar(s2[:, s % 2, :], s2[:, s % 2, :], REPLACED, None, ALU.is_le)\
                            .then_inc(sel_ready.sem, 1)
                        pool.wait_ge(exp2_ready.sem, exp2_ready.at(b, 2 * s + 2))
                        pool.wait_ge(sel_ready.sem, sel_ready.at(b, s + 1))
                        g.tensor_tensor(es[:, s % 3, :], es[:, s % 3, :], s2[:, s % 2, :], ALU.mult)\
                            .then_inc(p2_ready.sem, 1)
                    fill(("cross", s), a)
                fill("heads2", a)
                if b is not None:
                    inverse_deviation(b, stats1, 2, mv1, EPS1, rstd1, rstd1_ready)
                    plus_bias(b, 2, xs)
                fill("norm3", a)
                for j in range(HID // P) if b is not None else []:
                    pool.wait_ge(tanh1.sem, tanh1.at(b, j + 1))
                    alone()
                    g.tensor_scalar(thm[:, j % 4, :], thm[:, j % 4, :], 1.0, None, ALU.add).then_inc(plus1.sem, 1)

            iteration(0, None)
            iteration(1, 0)
            with pool.Fori(2, B) as i:
                iteration(i, i - 1)
            iteration(None, B - 1)

        @block.scalar
        def _(act):
            A = nc.scalar.activation
            act.wait_ge(raw_loaded, RAW_LOADED)
            A(cond_tanh[:, :, :], cond_col[:, :, :], ACT.Tanh, scale=0.5).then_inc(cond_tanh_ready, 1)
            act.wait_ge(setup_done, 1)

            def transposed(b, products, name, dst, signal_, waits=()):
                act.wait_ge(products.sem(name), products.at(b, name))
                A(dst, products.bank(name)[:, :].rearrange("p (a n) -> p a n", a=2), ACT.Copy).then_inc(signal_.sem, 1)

            def fill(slot, a):
                for name in FILL.get(slot, []) if a is not None else []:
                    if name == "ctxT":
                        transposed(a, L0, name, ctxT[:, :, :], ctxT_ready)
                        if later(a):
                            act.wait_ge(lgT_ready.sem, lgT_ready.at(a - 1))
                        A(rb[:, :], rout_bias[:, bass.ds(a, 1)], ACT.Copy).then_inc(rb_ready.sem, 1)
                    if name == "nxT":
                        act.wait_ge(L0.sem(name), L0.at(a, name))
                        for c in range(NC):
                            A(nxT[:, c, :], L0.bank(name)[:, c * T:(c + 1) * T], ACT.Identity,
                              bias=beta[:, c:c + 1], scale=gamma[:, c:c + 1]).then_inc(nxT_ready.sem, 1)
                    if name == "sc":
                        act.wait_ge(nm0_ready.sem, nm0_ready.at(a))
                        for t in range(NT):
                            A(p0[:, t, :], L0.bank(name)[:, t * T:(t + 1) * T], ACT.Exp, bias=nm0[:, t:t + 1],
                              accum_out=sum0[:, t:t + 1]).then_inc(exp0_ready.sem, 1)
                    if name == "PT":
                        transposed(a, L0, name, pT0[:, :, :], pT0_ready)
                    if name == "lgT":
                        act.wait_ge(L0.sem(name), L0.at(a, name))
                        act.wait_ge(rb_ready.sem, rb_ready.at(a))
                        A(lgT[:, :], L0.bank(name)[0:E, 0:T], ACT.Identity, bias=rb[:, :]).then_inc(lgT_ready.sem, 1)
                    if name == "lg":
                        act.wait_ge(router.sem, router.at(a, 2))
                        A(lexp[:, :, :], lsub[:, :, :], ACT.Exp).then_inc(lexp_ready.sem, 1)
                    if name[0] == "h":
                        j = int(name[1:])
                        act.wait_ge(L0.sem(name), L0.at(a, name))
                        act.wait_ge(hb_ready.sem, hb_ready.at(a))
                        if j >= 2:
                            act.wait_ge(hid_ready.sem, hid_ready.at(a, 2 * j - 2))
                        elif later(a):
                            act.wait_ge(hid_ready.sem, hid_ready.at(a - 1))
                        for u in range(2):
                            n = 2 * j + u
                            A(th[:, j % 2, u, :], L0.bank(name)[:, u * T:(u + 1) * T], ACT.Tanh,
                              bias=hb[:, NCH + n:NCH + n + 1], scale=0.5).then_inc(tanh0.sem, 1)
                    if name == "g":
                        act.wait_ge(zg_ready.sem, zg_ready.at(a))
                        A(zg[:, :, :], zg[:, :, :], ACT.Tanh, scale=0.5).then_inc(tg_ready.sem, 1)

            def normed(b, n):
                name = f"hT{n + 1}"
                act.wait_ge(L1.sem(name), L1.at(b, name))
                act.wait_ge(ad_ready.sem, ad_ready.at(b))
                for c in range(NC):
                    A(hT[:, c, :], L1.bank(name)[:, c * T:(c + 1) * T], ACT.Identity,
                      bias=ad[:, 4 * n + c:4 * n + c + 1], scale=ad[:, 4 * n + 2 + c:4 * n + 3 + c]).then_inc(hT_ready.sem, 1)

            def queries(b, name, bias):
                act.wait_ge(L1.sem(name), L1.at(b, name))
                for c in range(NC):
                    A(qT[:, c, :], L1.bank(name)[:, c * T:(c + 1) * T], ACT.Identity,
                      bias=bias[:, c:c + 1], scale=0.25).then_inc(q_ready.sem, 1)

            def weightsT(b, kind, g, et_ready, o_name, part):
                act.wait_ge(L1.sem((kind, g)), L1.at(b, (kind, g)))
                if g >= 2:
                    act.wait_ge(L1.sem(o_name), L1.at(b, o_name, part))
                A(et[:, g % 2, :], L1.bank((kind, g))[:, :], ACT.Copy).then_inc(et_ready.sem, 1)

            def iteration(a, b):
                if b is not None:
                    act.wait_ge(L1.sem("k2"), L1.at(b, "k2"))
                    if later(b):
                        act.wait_ge(km_ready.sem, km_ready.at(b - 1))
                    for c in range(NC):
                        A(kT2[:, c, :], L1.bank("k2")[:, c * T:(c + 1) * T], ACT.Identity, bias=bk2[:, c:c + 1])\
                            .then_inc(k2_ready.sem, 1)
                fill("start0", a)
                if b is not None:
                    normed(b, 0)
                fill("start1", a)
                if b is not None:
                    queries(b, "q1", bq1)
                for s in range(SELF_GROUPS + PV_LAG):
                    if b is not None and s < SELF_GROUPS:
                        act.wait_ge(max1_ready.sem, max1_ready.at(b, s + 1))
                        if s >= 3:
                            act.wait_ge(L1.sem(("T1", s - 3)), L1.at(b, ("T1", s - 3)))
                        for u in range(4):
                            A(es[:, s % 3, u * P:(u + 1) * P], L1.bank(("S1", s))[:, u * P:(u + 1) * P], ACT.Exp,
                              bias=nms[:, s % 2, u:u + 1]).then_inc(exp1_ready.sem, 1)
                    fill(("self", s), a)
                    g = s - S_LAG
                    if b is not None and 0 <= g < SELF_GROUPS:
                        weightsT(b, "T1", g, et1_ready, ("O1", (g - 2) // 4), (g - 2) % 4 + 1)
                fill("heads1", a)
                if b is not None:
                    transposed(b, L1, "oT1", oT[:, :, :], oT_ready)
                fill("norm2", a)
                if b is not None:
                    normed(b, 1)
                    queries(b, "q2", bq2)
                for s in range(CROSS_GROUPS + PV_LAG):
                    if b is not None and s < CROSS_GROUPS:
                        act.wait_ge(top.sem, top.at(b, 9 * s + 5))
                        if s >= 3:
                            act.wait_ge(L1.sem(("T2", s - 3)), L1.at(b, ("T2", s - 3)))
                        for u in range(2):
                            A(es[:, s % 3, u * T:(u + 1) * T], L1.bank(("S2", s))[:, u * T:(u + 1) * T], ACT.Exp,
                              bias=nmc[:, s % 2, u:u + 1]).then_inc(exp2_ready.sem, 1)
                    fill(("cross", s), a)
                    g = s - S_LAG
                    if b is not None and 0 <= g < CROSS_GROUPS:
                        weightsT(b, "T2", g, et2_ready, ("O2", (g - 2) // 8), (g - 2) % 8 + 1)
                fill("heads2", a)
                if b is not None:
                    transposed(b, L1, "oT2", oT[:, :, :], oT_ready)
                fill("norm3", a)
                if b is not None:
                    normed(b, 2)
                    for j in range(HID // P):
                        act.wait_ge(L1.sem(("m", j)), L1.at(b, ("m", j)))
                        if j >= 4:
                            act.wait_ge(mlp.sem, mlp.at(b, 2 * (j - 4) + 2))
                        A(thm[:, j % 4, :], L1.bank(("m", j))[:, 0:T], ACT.Tanh, bias=bm1_half[:, j:j + 1], scale=0.5)\
                            .then_inc(tanh1.sem, 1)

            iteration(0, None)
            iteration(1, 0)
            with act.Fori(2, B) as i:
                iteration(i, i - 1)
            iteration(None, B - 1)

        @block.vector
        def _(dve):
            v = nc.vector

            def alone():
                dve.nop(nofuse=True)

            done = [0]

            def step(ins):
                done[0] += 1
                ins.then_inc(setup_ev, 1)

            dve.wait_ge(cond_tanh_ready, 1)
            v.scalar_tensor_tensor(scond[:, :, :], cond_tanh[:, :, :], 1.0, cond_col[:, :, :], ALU.add, ALU.mult)\
                .then_inc(scond_ready, 1)
            dve.wait_ge(scond_ready, 1)
            v.tensor_scalar(scond[:, :, :], scond[:, :, :], 0.5, None, ALU.mult).then_inc(scond_ready, 1)
            v.tensor_copy(eb2_cols[:, :, :, :], eb2_col[:, :, :, :].broadcast_to([P, NC, E, P])).then_inc(scond_ready, 1)
            v.tensor_copy(bv_cols[:, :, :, :], bv_col[:, :, :, :].broadcast_to([P, NC, 2, B])).then_inc(scond_ready, 1)
            for i, p in enumerate(SETUP):
                bank, kind = banks[i % 2], p[0]
                dve.wait_ge(setup_mm, i + 1)
                if kind in ("tq", "tk", "tv"):
                    dst = {"tq": tq, "tk": tk, "tv": tv}[kind]
                    step(v.tensor_copy(dst[:, p[1], :], bank[:, 0:C]))
                elif kind == "tw2":
                    step(v.tensor_copy(tw2[:, :, 2 * P * p[1]:2 * P * (p[1] + 1)], bank[:, :].rearrange("p (c n) -> p c n", c=NC)))
                elif kind == "wqk":
                    step(v.tensor_scalar(wqk[:, p[1], :], bank[:, 0:C], float(C) ** -0.5, None, ALU.mult))
                elif kind == "ev":
                    n = min(512, W1_COLS - p[2])
                    step(v.tensor_copy(w1[:, NC + p[1], p[2]:p[2] + n], bank[:, 0:n]))
                elif kind == "w2":
                    step(v.tensor_scalar(w2[:, 2 * p[1]:2 * p[1] + 2, :], bank[:, :].rearrange("p (k n) -> p k n", k=2), 0.25, None, ALU.mult))
                elif kind == "eb2":
                    step(v.tensor_scalar(e_b2_all[:, p[1], :], bank[:, 0:C], 0.5, None, ALU.mult))
                elif kind == "hid":
                    step(v.tensor_tensor(hid_bias[:, :, 0:NCH].rearrange("p b j -> p j b"),
                                         bank[:, 0:NCH * B].rearrange("p (j b) -> p j b", j=NCH),
                                         hid_b.unsqueeze(2).broadcast_to([P, NCH, B]), ALU.add))
                elif kind == "rout":
                    step(v.tensor_scalar(rout_bias[:, :], bank[0:E, 0:B], rout_b[0:E, :], None, ALU.add))
                elif kind == "ada":
                    step(v.tensor_tensor(ada[:, :, :].rearrange("p b j -> p j b"),
                                         bank[:, 0:6 * NC * B].rearrange("p (j b) -> p j b", j=6 * NC),
                                         ada_b.unsqueeze(2).broadcast_to([P, 6 * NC, B]), ALU.add))
                elif kind == "gate":
                    step(v.tensor_tensor(mrow[0:B, 2 * p[1], :], bank[0:B, 0:C], gate_bias[0:B, p[1], :], ALU.add))
                elif kind == "bias":
                    step(v.tensor_tensor(row_bias[0:B, p[1], :], bank[0:B, 0:C], row_bias[0:B, p[1], :], ALU.add))
            dve.wait_ge(setup_ev, len(SETUP))
            dve.wait_ge(weights_loaded, WEIGHTS_LOADED)
            v.tensor_tensor(mrow[0:B, 1:6:2, :], row_bias[0:B, :, :], mrow[0:B, 0:6:2, :], ALU.mult).then_inc(rows_ready, 1)
            v.tensor_scalar(hid_bias[:, :, NCH:], hid_bias[:, :, 0:NCH], 0.5, None, ALU.mult).then_inc(scond_ready, 1)
            for n in range(3):
                w = ada[:, :, 4 * n + 2:4 * n + 4]
                v.tensor_scalar(w, w, 1.0, None, ALU.add).then_inc(scond_ready, 1)
            for w, s in ((wg2[:, :, :], 0.5), (wm2[:, :, :], 0.5), (out_b_all[:, :], 0.5), (bq1[:, :], 0.25), (bq2[:, :], 0.25)):
                v.tensor_scalar(w, w, s, None, ALU.mult).then_inc(scond_ready, 1)
            v.tensor_scalar(bm1_half[:, :], bm1[:, 0:HID // P], 0.5, None, ALU.mult).then_inc(scond_ready, 1)
            dve.wait_ge(scond_ready, 14)
            dve.wait_ge(rows_ready, 1)
            dve.wait_ge(rows_stored, 16)
            v.tensor_copy(hb[:, 0:1], bm1[:, 0:1]).then_inc(setup_done, 1)
            dve.wait_ge(setup_done, 1)

            def norm(b, x_, stats, n0, st, mv, rstd, rstd_ready, dst, ready):
                for t in range(NT):
                    v.bn_stats(st[:, t, :], x_[:, t, :]).then_inc(stats.sem, 1)
                dve.wait_ge(stats.sem, stats.at(b, n0 + 2))
                alone()
                for t in range(NT):
                    v.bn_aggr(mv[:, t, :], st[:, t, :]).then_inc(stats.sem, 1)
                dve.wait_ge(stats.sem, stats.at(b, n0 + 4))
                dve.wait_ge(rstd_ready.sem, rstd_ready.at(b, n0 // 2 + 2))
                for t in range(NT):
                    v.tensor_scalar(dst[:, t, :], x_[:, t, :], mv[:, t, 0:1], rstd[:, t, :], ALU.subtract, ALU.mult)\
                        .then_inc(ready.sem, 1)

            def fill(slot, a):
                for name in FILL.get(slot, []) if a is not None else []:
                    if name in L0.of and name not in ("ctxT", "nxT", "sc", "PT", "lgT") and name[0] != "h":
                        dve.wait_ge(L0.sem(name), L0.at(a, name))
                    if name == "nxT":
                        dve.wait_ge(x_loaded.sem, x_loaded.at(a))
                        if later(a):
                            dve.wait_ge(L0.sem("PT"), L0.at(a - 1, "PT"))
                        norm(a, x_in, stats0, 0, st0, mv0, rstd0, rstd0_ready, nx, nx_ready)
                        if later(a):
                            dve.wait_ge(tanh0.sem, tanh0.at(a - 1))
                            dve.wait_ge(hid_ready.sem, hid_ready.at(a - 1))
                        v.tensor_copy(hb[:, :].unsqueeze(1), hid_bias[:, bass.ds(a, 1), :]).then_inc(hb_ready.sem, 1)
                    if name == "kp":
                        v.tensor_copy(kpT[:, :, :], L0.bank(name)[:, :].rearrange("p (c t) -> p c t", c=NC)).then_inc(kp_ready.sem, 1)
                    if name == "sc":
                        dve.wait_ge(L0.sem(name), L0.at(a, name))
                        v.tensor_reduce(nm0[:, :], L0.bank(name)[:, :].rearrange("p (t k) -> p t k", t=NT),
                                        axis=AX_X, op=ALU.max, negate=True).then_inc(nm0_ready.sem, 1)
                        dve.wait_ge(exp0_ready.sem, exp0_ready.at(a))
                        v.reciprocal(r0[:, :], sum0[:, :]).then_inc(r0_ready.sem, 1)
                    if name == "evT":
                        v.tensor_copy(evT[:, :, :], L0.bank(name)[:, :].rearrange("p (c t) -> p c t", c=NC)).then_inc(evT_ready.sem, 1)
                    if name == "lg":
                        lg = L0.bank(name)[:, 0:4 * NT].rearrange("p (t e) -> p t e", t=NT)[:, :, 0:E]
                        v.tensor_reduce(lmax[:, :, 0], lg, axis=AX_X, op=ALU.max).then_inc(router.sem, 1)
                        dve.wait_ge(router.sem, router.at(a, 1))
                        v.tensor_tensor(lsub[:, :, :], lg, lmax[:, :, :].broadcast_to([P, NT, E]), ALU.subtract).then_inc(router.sem, 1)
                        dve.wait_ge(lexp_ready.sem, lexp_ready.at(a))
                        v.tensor_reduce(lsum[:, :, 0], lexp[:, :, :], axis=AX_X, op=ALU.add).then_inc(router.sem, 1)
                        dve.wait_ge(router.sem, router.at(a, 3))
                        v.reciprocal(lrec[:, :, :], lsum[:, :, :]).then_inc(router.sem, 1)
                        dve.wait_ge(router.sem, router.at(a, 4))
                        v.tensor_tensor(prob[:, :, :], lexp[:, :, :], lrec[:, :, :].broadcast_to([P, NT, E]), ALU.mult).then_inc(router.sem, 1)
                        dve.wait_ge(router.sem, router.at(a, 5))
                        for e in range(E):
                            if e:
                                dve.wait_ge(mix.sem, mix.at(a, 2 * e))
                            for t in range(NT):
                                v.scalar_tensor_tensor(acc[:, t, :], e_b2_all[:, e, :], prob[:, t, e:e + 1],
                                                       acc[:, t, :] if e else out_b_all[:, :], ALU.mult, ALU.add)\
                                    .then_inc(mix.sem, 1)
                    if name[0] == "h":
                        j = int(name[1:])
                        if j == 0 and later(a):
                            dve.wait_ge(L0.sem("y1"), L0.at(a - 1, "y1"))
                            dve.wait_ge(L0.sem("y2"), L0.at(a - 1, "y2"))
                        if j == 0:
                            dve.wait_ge(hb_ready.sem, hb_ready.at(a))
                        dve.wait_ge(plus0.sem, plus0.at(a, j + 1))
                        for u in range(2):
                            n = 2 * j + u
                            v.scalar_tensor_tensor(hid[:, n, :], L0.bank(name)[:, u * T:(u + 1) * T], hb[:, n:n + 1],
                                                   th[:, j % 2, u, :], ALU.add, ALU.mult).then_inc(hid_ready.sem, 1)
                    if name == "g":
                        v.tensor_tensor(zg[:, :, :], L0.bank(name)[:, :].rearrange("p (t c) -> p t c", t=NT),
                                        gate_b2_all[:, :, :].broadcast_to([P, NT, C]), ALU.add).then_inc(zg_ready.sem, 1)
                    if name[0] == "y":
                        e = int(name[1:])
                        dve.wait_ge(mix.sem, mix.at(a, 6 + 2 * e))
                        for t in range(NT):
                            v.scalar_tensor_tensor(acc[:, t, :], L0.bank(name)[:, t * C:(t + 1) * C], prob[:, t, e:e + 1],
                                                   acc[:, t, :], ALU.mult, ALU.add).then_inc(mix.sem, 1)
                        if e == E - 1:
                            dve.wait_ge(mix.sem, mix.at(a))
                            dve.wait_ge(tg_ready.sem, tg_ready.at(a))
                            v.scalar_tensor_tensor(acc[:, :, :], zg[:, :, :], 1.0, acc[:, :, :], ALU.add, ALU.mult)\
                                .then_inc(x1_ready.sem, 1)
                            dve.wait_ge(x1_ready.sem, x1_ready.at(a, 1))
                            dve.wait_ge(x_copied.sem, x_copied.at(a))
                            if later(a):
                                dve.wait_ge(xb_ready.sem, xb_ready.at(a - 1, 1))
                            v.tensor_tensor(x1[:, :, :], acc[:, :, :], x_res[:, :, :], ALU.add).then_inc(x1_ready.sem, 1)

            def norm1(b, n, src):
                if n:
                    dve.wait_ge(xs_ready.sem, xs_ready.at(b, n))
                else:
                    dve.wait_ge(x1_ready.sem, x1_ready.at(b))
                    if later(b):
                        dve.wait_ge(hT_ready.sem, hT_ready.at(b - 1))
                norm(b, src, stats1, 4 * n, st1, mv1, rstd1, rstd1_ready, xn, xn_ready)

            def values(b, name, va, ready):
                dve.wait_ge(L1.sem(name), L1.at(b, name))
                if later(b):
                    dve.wait_ge(o_ready.sem, o_ready.at(b - 1))
                for t in range(NT):
                    v.tensor_copy(va[:, t, :, 0:D], L1.bank(name)[:, t * C:(t + 1) * C].rearrange("p (h d) -> p h d", h=H))\
                        .then_inc(ready.sem, 1)

            def heads(b, name, w, n0, parts):
                sums = L1.bank((name, w))[:, 0:H * VA].rearrange("p (h d) -> p h d", h=H)
                dve.wait_ge(L1.sem((name, w)), L1.at(b, (name, w), parts))
                v.reciprocal(ro[:, w, :, :], sums[:, :, D:VA]).then_inc(ro_ready.sem, 1)
                dve.wait_ge(ro_ready.sem, ro_ready.at(b, n0 + w + 1))
                v.tensor_tensor(o[:, w, :].rearrange("p (h d) -> p h d", h=H), sums[:, :, 0:D],
                                ro[:, w, :, :].broadcast_to([P, H, D]), ALU.mult).then_inc(o_ready.sem, 1)

            def residual(b, name, s):
                dve.wait_ge(L1.sem(name), L1.at(b, name))
                if s == 0:
                    dve.wait_ge(grow_loaded.sem, grow_loaded.at(b))
                v.tensor_tensor(tmp[:, :, :], L1.bank(name)[:, :].rearrange("p (t c) -> p t c", t=NT),
                                grow[:, 2 * s:2 * s + 1, :].broadcast_to([P, NT, C]), ALU.mult).then_inc(gy_ready.sem, 1)
                dve.wait_ge(gy_ready.sem, gy_ready.at(b, s + 1))
                dve.wait_ge(xb_ready.sem, xb_ready.at(b, s + 1))
                if s == 0 and later(b):
                    dve.wait_ge(stored.sem, stored.at(b - 1))
                v.tensor_tensor(xs[:, :, :], tmp[:, :, :], xb[:, :, :], ALU.add).then_inc(xs_ready.sem, 1)

            def top16(b, g):
                S, r = L1.bank(("S2", g)), g % 2
                dve.wait_ge(L1.sem(("S2", g)), L1.at(b, ("S2", g)))
                alone()
                for u in range(2):
                    v.max(m8[:, r, u, :], S[:, u * T:(u + 1) * T]).then_inc(top.sem, 1)
                dve.wait_ge(top.sem, top.at(b, 9 * g + 2))
                v.tensor_scalar(nmc[:, r, :], m8[:, r, 0:2, 0], -1.0, None, ALU.mult).then_inc(top.sem, 1)
                for u in range(2):
                    v.match_replace(s1[:, u * T:(u + 1) * T], m8[:, r, u, :], S[:, u * T:(u + 1) * T], REPLACED)\
                        .then_inc(top.sem, 1)
                dve.wait_ge(top.sem, top.at(b, 9 * g + 5))
                alone()
                for u in range(2):
                    v.max(m8[:, r, 2 + u, :], s1[:, u * T:(u + 1) * T]).then_inc(top.sem, 1)
                if g >= 2:
                    dve.wait_ge(p2_ready.sem, p2_ready.at(b, g - 1))
                dve.wait_ge(top.sem, top.at(b, 9 * g + 7))
                alone()
                for u in range(2):
                    v.match_replace(s2[:, r, u * T:(u + 1) * T], m8[:, r, 2 + u, :], s1[:, u * T:(u + 1) * T], REPLACED)\
                        .then_inc(top.sem, 1)

            def iteration(a, b):
                if b is not None:
                    norm1(b, 0, x1)
                    if later(b):
                        dve.wait_ge(hT_ready.sem, hT_ready.at(b - 1))
                    v.tensor_copy(ad[:, :].unsqueeze(1), ada[:, bass.ds(b, 1), :]).then_inc(ad_ready.sem, 1)
                    dve.wait_ge(ones_ready, 2)
                    values(b, "v2", va2, va2_ready)
                fill("start0", a)
                fill("start1", a)
                if b is not None:
                    dve.wait_ge(L1.sem("k1"), L1.at(b, "k1"))
                    for c in range(NC):
                        v.tensor_scalar(kT1[:, c, :], L1.bank("k1")[:, c * T:(c + 1) * T], bk1[:, c:c + 1], None, ALU.add)\
                            .then_inc(k1_ready.sem, 1)
                    values(b, "v1", va1, va1_ready)
                for s in range(SELF_GROUPS + PV_LAG):
                    if b is not None and s < SELF_GROUPS:
                        dve.wait_ge(L1.sem(("S1", s)), L1.at(b, ("S1", s)))
                        v.tensor_reduce(nms[:, s % 2, :], L1.bank(("S1", s))[:, :].rearrange("p (h k) -> p h k", h=4),
                                        axis=AX_X, op=ALU.max, negate=True).then_inc(max1_ready.sem, 1)
                    fill(("self", s), a)
                if b is not None:
                    for w in range(2):
                        heads(b, "O1", w, 0, 4)
                fill("heads1", a)
                if b is not None:
                    residual(b, "so", 0)
                    norm1(b, 1, xs)
                fill("norm2", a)
                for s in range(CROSS_GROUPS + PV_LAG):
                    if b is not None and s < CROSS_GROUPS:
                        top16(b, s)
                    fill(("cross", s), a)
                if b is not None:
                    for t in range(NT):
                        heads(b, "O2", t, 2, 8)
                fill("heads2", a)
                if b is not None:
                    residual(b, "co", 1)
                    norm1(b, 2, xs)
                fill("norm3", a)
                if b is not None:
                    for j in range(HID // P):
                        bank = L1.bank(("m", j))
                        dve.wait_ge(plus1.sem, plus1.at(b, j + 1))
                        v.scalar_tensor_tensor(thm[:, j % 4, :], bank[:, 0:T], bm1[:, j:j + 1], thm[:, j % 4, :],
                                               ALU.add, ALU.mult).then_inc(mlp.sem, 1)
                        dve.wait_ge(mlp.sem, mlp.at(b, 2 * j + 1))
                        v.scalar_tensor_tensor(gated[:, j, :], bank[:, T:2 * T], bm1[:, HID // P + j:HID // P + j + 1],
                                               thm[:, j % 4, :], ALU.add, ALU.mult).then_inc(mlp.sem, 1)
                    residual(b, "y", 2)

            iteration(0, None)
            iteration(1, 0)
            with dve.Fori(2, B) as i:
                iteration(i, i - 1)
            iteration(None, B - 1)

        @block.tensor
        def _(pe):
            def mm(out_, lhsT, rhs, k, n):
                return nc.tensor.matmul(out_, lhsT, rhs, start=(k == 0), stop=(k == n - 1))

            pe.wait_ge(ident_ready, 1)
            pe.wait_ge(raw_loaded, RAW_LOADED)
            pe.wait_ge(scond_ready, 4)
            for i, p in enumerate(SETUP):
                bank, kind = banks[i % 2], p[0]
                if i >= 2:
                    pe.wait_ge(setup_ev, i - 1)
                if kind in ("tq", "tk", "tv"):
                    src = {"tq": raw_q, "tk": raw_k, "tv": raw_v}[kind]
                    for c in range(NC):
                        last = nc.tensor.transpose(bank[:, c * P:(c + 1) * P], src[:, c, p[1] * P:(p[1] + 1) * P], ident[:, :])
                elif kind == "tw2":
                    for k in range(2):
                        for c in range(NC):
                            last = nc.tensor.transpose(bank[:, c * 2 * P + k * P:c * 2 * P + (k + 1) * P],
                                                       w2[:, 2 * p[1] + k, c * P:(c + 1) * P], ident[:, :])
                elif kind == "wqk":
                    if p[1] == 0:
                        pe.wait_ge(setup_ev, SETUP.index(("tw2", 5)) + 1)
                    for k in range(NC):
                        last = mm(bank[:, 0:C], tk[:, k, p[1] * P:(p[1] + 1) * P], tq[:, k, :], k, NC)
                elif kind == "ev":
                    n = min(512, W1_COLS - p[2])
                    for k in range(NC):
                        last = mm(bank[:, 0:n], tv[:, k, p[1] * P:(p[1] + 1) * P], raw_ev[:, k, p[2]:p[2] + n], k, NC)
                elif kind == "w2":
                    for u in range(2):
                        for k in range(NC):
                            f = (2 * p[1] + u) * P
                            last = mm(bank[:, u * C:(u + 1) * C], tw2[:, k, f:f + P], raw_o[:, k, :], k, NC)
                elif kind == "eb2":
                    for k in range(NC):
                        last = mm(bank[:, 0:C], eb2_cols[:, k, p[1], :], raw_o[:, k, :], k, NC)
                elif kind == "hid":
                    for j in range(NCH):
                        for k in range(NC):
                            last = mm(bank[:, j * B:(j + 1) * B], raw_an[:, k, j * P:(j + 1) * P], cond_col[:, k, :], k, NC)
                elif kind == "rout":
                    for k in range(NC):
                        last = mm(bank[0:E, 0:B], raw_an[:, k, ROUT_COL:W1_COLS], cond_col[:, k, :], k, NC)
                elif kind == "ada":
                    for j in range(6 * NC):
                        n, u = j // 4, j % 4
                        for k in range(NC):
                            lo = 3 * n * C + u * P
                            last = mm(bank[:, j * B:(j + 1) * B], raw_ada[:, k, lo:lo + P], scond[:, k, :], k, NC)
                elif kind == "gate":
                    for k in range(NC):
                        lo = (3 * p[1] + 2) * C
                        last = mm(bank[0:B, 0:C], scond[:, k, :], raw_ada[:, k, lo:lo + C], k, NC)
                elif kind == "bias":
                    if p[1] == 0:
                        pe.wait_ge(weights_loaded, WEIGHTS_LOADED)
                    for k in range(NC):
                        last = mm(bank[0:B, 0:C], bv_cols[:, k, p[1], :], (wso, wco)[p[1]][:, k, :], k, NC)
                last.then_inc(setup_mm, 1)
            pe.wait_ge(setup_done, 1)

            def transpose4(bank, src):
                for c in range(2):
                    for t in range(2):
                        last = nc.tensor.transpose(bank[:, c * T + t * P:c * T + (t + 1) * P],
                                                   src[:, t, c * P:(c + 1) * P], ident[:, :])
                return last

            def by_channel(bank, w, lo, actT, n=NC):
                for c in range(2):
                    for k in range(n):
                        last = mm(bank[:, c * T:(c + 1) * T], w[:, k, lo + c * P:lo + (c + 1) * P], actT[:, k, :], k, n)
                return last

            def by_token(bank, actT, w, lo, n=NC, k0=0):
                for t in range(NT):
                    for k in range(n):
                        last = mm(bank[:, t * C:(t + 1) * C], actT[:, k0 + k, t * P:(t + 1) * P], w[:, k0 + k, lo:lo + C], k, n)
                return last

            def comb(k):
                return nxT[:, k, :] if k < NC else evT[:, k - NC, :]

            def fill(slot, a):
                for name in FILL.get(slot, []) if a is not None else []:
                    bank = L0.bank(name)
                    if name == "ctxT":
                        if later(a):
                            pe.wait_ge(mix.sem, mix.at(a - 1))
                        pe.wait_ge(ctx_loaded.sem, ctx_loaded.at(a))
                        alone()
                        last = transpose4(bank, ctx_in)
                    if name == "nxT":
                        pe.wait_ge(nx_ready.sem, nx_ready.at(a))
                        last = transpose4(bank, nx)
                    if name == "kp":
                        pe.wait_ge(ctxT_ready.sem, ctxT_ready.at(a))
                        last = by_channel(bank, wqk, 0, ctxT)
                    if name == "sc":
                        pe.wait_ge(nxT_ready.sem, nxT_ready.at(a))
                        pe.wait_ge(kp_ready.sem, kp_ready.at(a))
                        last = by_token(bank, nxT, kpT, 0)
                    if name == "PT":
                        pe.wait_ge(p0_ready.sem, p0_ready.at(a))
                        last = transpose4(bank, p0)
                    if name == "evT":
                        pe.wait_ge(exp0_ready.sem, exp0_ready.at(a))
                        pe.wait_ge(pT0_ready.sem, pT0_ready.at(a))
                        last = by_channel(bank, ctx_in, 0, pT0)
                    if name == "lgT":
                        pe.wait_ge(evT_ready.sem, evT_ready.at(a))
                        for k in range(2 * NC):
                            last = mm(bank[0:E, 0:T], w1[:, k, ROUT_COL:W1_COLS], comb(k), k, 2 * NC)
                    if name == "lg":
                        pe.wait_ge(lgT_ready.sem, lgT_ready.at(a))
                        alone()
                        for t in range(NT):
                            last = nc.tensor.transpose(bank[:, 4 * t:4 * t + E], lgT[:, t * P:(t + 1) * P], ident[0:E, 0:E])
                    if name[0] == "h":
                        j = int(name[1:])
                        if j == 1:
                            pe.wait_ge(router.sem, router.at(a, 2))
                        if j >= 2:
                            pe.wait_ge(hid_ready.sem, hid_ready.at(a, 2 * j - 2))
                        for u in range(2):
                            for k in range(2 * NC):
                                lo = (2 * j + u) * P
                                last = mm(bank[:, u * T:(u + 1) * T], w1[:, k, lo:lo + P], comb(k), k, 2 * NC)
                    if name == "g":
                        pe.wait_ge(hid_ready.sem, hid_ready.at(a))
                        for t in range(NT):
                            for k in range(NC):
                                last = mm(bank[:, t * C:(t + 1) * C], hid[:, EXP_COLS // P + k, t * P:(t + 1) * P], wg2[:, k, :], k, NC)
                    if name[0] == "y":
                        if name == "y1":
                            pe.wait_ge(zg_ready.sem, zg_ready.at(a))
                        if name == "y2":
                            pe.wait_ge(mix.sem, mix.at(a, 8))
                        last = by_token(bank, hid, w2, 0, RH // P, int(name[1:]) * (RH // P))
                    last.then_inc(L0.sem(name), 1)

            def alone():
                pe.nop(nofuse=True)

            def self_scores(b, g):
                w, q = g // 4, g % 4
                if g == 0:
                    pe.wait_ge(q_ready.sem, q_ready.at(b, 2))
                if g >= 2:
                    pe.wait_ge(exp1_ready.sem, exp1_ready.at(b, 4 * g - 4))
                pe.wait_ge(km_ready.sem, km_ready.at(b, 4 * q + 4))
                mm(L1.bank(("S1", g))[:, :].rearrange("p (h k) -> p h k", h=4), qT[:, q // 2, w * P:(w + 1) * P],
                   KM[:, 4 * q:4 * q + 4, w * P:(w + 1) * P], 0, 1).then_inc(L1.sem(("S1", g)), 1)

            def self_transposes(b, g):
                if g == 1:
                    pe.wait_ge(va1_ready.sem, va1_ready.at(b))
                if g >= 2:
                    pe.wait_ge(et1_ready.sem, et1_ready.at(b, g - 1))
                pe.wait_ge(exp1_ready.sem, exp1_ready.at(b, 4 * g + 4))
                for u in range(4):
                    last = nc.tensor.transpose(L1.bank(("T1", g))[:, u * P:(u + 1) * P], es[:, g % 3, u * P:(u + 1) * P], ident[:, :])
                last.then_inc(L1.sem(("T1", g)), 1)

            def self_pv(b, g):
                w, q = g // 4, g % 4
                if g == 0 and later(b):
                    pe.wait_ge(gy_ready.sem, gy_ready.at(b - 1))
                if g == 4 and later(b):
                    pe.wait_ge(o_ready.sem, o_ready.at(b - 1))
                pe.wait_ge(et1_ready.sem, et1_ready.at(b, g + 1))
                if g == 0:
                    pe.wait_ge(va1_ready.sem, va1_ready.at(b))
                for u in range(4):
                    h = 4 * q + u
                    last = mm(L1.bank(("O1", w))[:, h * VA:(h + 1) * VA], et[:, g % 2, u * P:(u + 1) * P], va1[:, w, h, :], 0, 1)
                last.then_inc(L1.sem(("O1", w)), 1)

            def cross_scores(b, g):
                t, p = g // 8, g % 8
                if g == 0:
                    pe.wait_ge(q_ready.sem, q_ready.at(b, 4))
                if g >= 2:
                    pe.wait_ge(exp2_ready.sem, exp2_ready.at(b, 2 * g - 2))
                pe.wait_ge(km_ready.sem, km_ready.at(b, H + 2 * p + 2))
                mm(L1.bank(("S2", g))[:, :].rearrange("p (h k) -> p h k", h=2), qT[:, p // 4, t * P:(t + 1) * P],
                   KM[:, 2 * p:2 * p + 2, :], 0, 1).then_inc(L1.sem(("S2", g)), 1)

            def cross_transposes(b, g):
                if g >= 2:
                    pe.wait_ge(et2_ready.sem, et2_ready.at(b, g - 1))
                pe.wait_ge(p2_ready.sem, p2_ready.at(b, g + 1))
                for u in range(4):
                    last = nc.tensor.transpose(L1.bank(("T2", g))[:, u * P:(u + 1) * P], es[:, g % 3, u * P:(u + 1) * P], ident[:, :])
                last.then_inc(L1.sem(("T2", g)), 1)

            def cross_pv(b, g):
                t, p = g // 8, g % 8
                pe.wait_ge(et2_ready.sem, et2_ready.at(b, g + 1))
                if g == 0:
                    pe.wait_ge(va2_ready.sem, va2_ready.at(b))
                for u in range(2):
                    h = 2 * p + u
                    for k in range(NT):
                        last = mm(L1.bank(("O2", t))[:, h * VA:(h + 1) * VA], et[:, g % 2, (2 * u + k) * P:(2 * u + k + 1) * P],
                                  va2[:, k, h, :], k, NT)
                last.then_inc(L1.sem(("O2", t)), 1)

            def attention(a, b, kind, groups, scores, transposes, pv):
                for s in range(groups + PV_LAG):
                    if b is not None and s < groups:
                        scores(b, s)
                    fill((kind, s), a)
                    if b is not None and 0 <= s - S_LAG < groups:
                        transposes(b, s - S_LAG)
                    if b is not None and 0 <= s - PV_LAG < groups:
                        pv(b, s - PV_LAG)

            def iteration(a, b):
                if b is not None:
                    pe.wait_ge(ctxT_ready.sem, ctxT_ready.at(b))
                    by_channel(L1.bank("k2"), wkv, 0, ctxT).then_inc(L1.sem("k2"), 1)
                    by_token(L1.bank("v2"), ctxT, wkv, C).then_inc(L1.sem("v2"), 1)
                fill("start0", a)
                if b is not None:
                    pe.wait_ge(xn_ready.sem, xn_ready.at(b, 2))
                    transpose4(L1.bank("hT1"), xn).then_inc(L1.sem("hT1"), 1)
                fill("start1", a)
                if b is not None:
                    pe.wait_ge(hT_ready.sem, hT_ready.at(b, 2))
                    pe.wait_ge(k2_ready.sem, k2_ready.at(b))
                    by_channel(L1.bank("q1"), wqkv, 0, hT).then_inc(L1.sem("q1"), 1)
                    pe.wait_ge(va2_ready.sem, va2_ready.at(b))
                    by_channel(L1.bank("k1"), wqkv, C, hT).then_inc(L1.sem("k1"), 1)
                    by_token(L1.bank("v1"), hT, wqkv, 2 * C).then_inc(L1.sem("v1"), 1)
                attention(a, b, "self", SELF_GROUPS, self_scores, self_transposes, self_pv)
                fill("heads1", a)
                if b is not None:
                    pe.wait_ge(o_ready.sem, o_ready.at(b, 2))
                    transpose4(L1.bank("oT1"), o).then_inc(L1.sem("oT1"), 1)
                    pe.wait_ge(oT_ready.sem, oT_ready.at(b, 1))
                    by_token(L1.bank("so"), oT, wso, 0).then_inc(L1.sem("so"), 1)
                fill("norm2", a)
                if b is not None:
                    pe.wait_ge(xn_ready.sem, xn_ready.at(b, 4))
                    transpose4(L1.bank("hT2"), xn).then_inc(L1.sem("hT2"), 1)
                    pe.wait_ge(hT_ready.sem, hT_ready.at(b, 4))
                    pe.wait_ge(gy_ready.sem, gy_ready.at(b, 1))
                    by_channel(L1.bank("q2"), wq2, 0, hT).then_inc(L1.sem("q2"), 1)
                attention(a, b, "cross", CROSS_GROUPS, cross_scores, cross_transposes, cross_pv)
                fill("heads2", a)
                if b is not None:
                    pe.wait_ge(o_ready.sem, o_ready.at(b, 4))
                    transpose4(L1.bank("oT2"), o).then_inc(L1.sem("oT2"), 1)
                    pe.wait_ge(oT_ready.sem, oT_ready.at(b, 2))
                    by_token(L1.bank("co"), oT, wco, 0).then_inc(L1.sem("co"), 1)
                fill("norm3", a)
                if b is not None:
                    pe.wait_ge(xn_ready.sem, xn_ready.at(b, 6))
                    transpose4(L1.bank("hT3"), xn).then_inc(L1.sem("hT3"), 1)
                    for j in range(HID // P):
                        name = ("m", j)
                        if j == 0:
                            pe.wait_ge(hT_ready.sem, hT_ready.at(b, 6))
                        if j == 2:
                            pe.wait_ge(gy_ready.sem, gy_ready.at(b, 2))
                        if j >= 4:
                            pe.wait_ge(mlp.sem, mlp.at(b, 2 * j - 6))
                        for u in range(2):
                            for k in range(NC):
                                lo = u * HID + j * P
                                last = mm(L1.bank(name)[:, u * T:(u + 1) * T], wm1[:, k, lo:lo + P], hT[:, k, :], k, NC)
                        last.then_inc(L1.sem(name), 1)
                    pe.wait_ge(mlp.sem, mlp.at(b))
                    by_token(L1.bank("y"), gated, wm2, 0, HID // P).then_inc(L1.sem("y"), 1)

            iteration(0, None)
            iteration(1, 0)
            with pe.Fori(2, B) as i:
                iteration(i, i - 1)
            iteration(None, B - 1)

    return nc


_L0 = ["ln_gamma", "ln_beta", "Wq", "Wk", "Wv", "router_W", "router_b", "e_w1", "e_b1", "e_w2", "e_b2",
       "gate_w1", "gate_b1", "gate_w2", "gate_b2", "out_w", "out_b"]
_L1 = ["w_ada", "b_ada", "w_qkv", "b_qkv", "w_so", "b_so", "w_q", "b_q", "w_kv", "b_kv", "w_co", "b_co",
       "w_m1", "b_m1", "w_m2", "b_m2"]
_INS = ["x", "cond_1024", "ctx_1024"] + ["L0_xcond_" + n for n in _L0] + ["L1_xcond_" + n for n in _L1]


def kernel(**inputs):
    import numpy as _np
    import concourse.bacc as _bacc
    from concourse.bass_utils import run_bass_kernel_spmd as _run

    nc = _bacc.Bacc("TRN2", target_bir_lowering=False, num_devices=1)
    arrays, args = {}, []
    for name in _INS:
        a = _np.ascontiguousarray(inputs[name])
        arrays[f"in_{name}_dram"] = a
        args.append(nc.dram_tensor(f"in_{name}_dram", a.shape, mybir.dt.from_np(a.dtype), kind="ExternalInput").ap())
    args.append(nc.dram_tensor("out_dram", (B, T, C), F32, kind="ExternalOutput").ap())
    build(nc, *args)
    r = _run(nc, [arrays], core_ids=[0])
    return r.results[0]["out_dram"]
```

```python
import concourse.bass as bass
from concourse import mybir
from contextlib import ExitStack

F32 = mybir.dt.float32
ALU = mybir.AluOpType
ACT = mybir.ActivationFunctionType
AX_X = mybir.AxisListType.X

P = 128
B, T, C = 16, 256, 256
NT, NC = T // P, C // P
E, RH = 3, 512
H, D = 16, 16
HPT = P // D
SHIFT = 64
WIN = 128
TOPK = 16
HID = 1024
EXP_COLS = E * RH
GATE_COL = EXP_COLS
ROUT_COL = GATE_COL + C
W1_COLS = ROUT_COL + E
NCH = (EXP_COLS + C) // P
EPS0, EPS1 = 1e-5, 1e-6
REPLACED = -3.0e38
VA = D + 1

SELF_GROUPS = 8
CROSS_GROUPS = 16
S_LAG, PV_LAG = 2, 4
FILL = {
    "norm3": ["nx", "ctxT"], ("mlp", 2): ["nxT", "kp"], ("mlp", 3): ["sc"], ("mlp", 7): ["PT"],
    "silu": ["evT"], "keys1": ["lgT"], ("self", 0): ["lg", "h0", "h1", "h2"], "heads1": ["h3"],
    "norm2": ["h4"], "proj2": ["h5"], ("cross", 0): ["h6"], ("cross", 2): ["h7", "h8"], ("cross", 4): ["h9"],
    ("cross", 6): ["h10"], ("cross", 7): ["h11"], ("cross", 9): ["h12", "h13"], ("cross", 13): ["g"],
    ("cross", 15): ["y0", "y1"], ("cross", 17): ["y2"], "heads2": ["y3"], "end": ["y4", "y5"],
}
NORM1_STEP = 2


class Signal:

    def __init__(self, sem, per):
        self.sem, self.per = sem, per

    def at(self, b, n=None):
        return b * self.per + (self.per if n is None else n)


class Products:

    def __init__(self, plan, banks, written):
        self.banks, self.written = banks, written
        self.of, self.count = {}, [0] * len(banks)
        for name, k, raises in plan:
            self.of[name] = (k, self.count[k])
            self.count[k] += raises

    def bank(self, name):
        return self.banks[self.of[name][0]]

    def sem(self, name):
        return self.written[self.of[name][0]]

    def at(self, b, name, part=1):
        k, before = self.of[name]
        return b * self.count[k] + before + part


def later(b):
    return not (isinstance(b, int) and b == 0)


def build(nc, x, cond_1024, ctx_1024, ln_gamma, ln_beta, Wq, Wk, Wv, router_W, router_b, e_w1, e_b1, e_w2,
          e_b2, gate_w1, gate_b1, gate_w2, gate_b2, out_w, out_b, w_ada, b_ada, w_qkv, b_qkv, w_so, b_so,
          w_q, b_q, w_kv, b_kv, w_co, b_co, w_m1, b_m1, w_m2, b_m2, out):
    ctx = ExitStack()
    with ctx:
        def sb(name, shape, dt=F32):
            return ctx.enter_context(nc.sbuf_tensor(name, shape, dt))

        def sem(name):
            return ctx.enter_context(nc.semaphore(name))

        def signal(name, per):
            return Signal(sem(name), per)

        ident = sb("ident", [P, P])
        wqk = sb("wqk", [P, NC, C])
        w1 = sb("w1", [P, 2 * NC, W1_COLS])
        w2 = sb("w2", [P, EXP_COLS // P, C])
        wg2 = sb("wg2", [P, NC, C])
        wqkv = sb("wqkv", [P, NC, 3 * C])
        wso = sb("wso", [P, NC, C])
        wq2 = sb("wq2", [P, NC, C])
        wkv = sb("wkv", [P, NC, 2 * C])
        wco = sb("wco", [P, NC, C])
        wm1 = sb("wm1", [P, NC, 2 * HID])
        wm2 = sb("wm2", [P, HID // P, C])
        gamma = sb("gamma", [P, NC])
        beta = sb("beta", [P, NC])
        gate_b2_all = sb("gate_b2_all", [P, 1, C])
        out_b_all = sb("out_b_all", [P, C])
        e_b2_all = sb("e_b2_all", [P, E, C])
        bq1 = sb("bq1", [P, NC])
        bk1 = sb("bk1", [P, NC])
        bq2 = sb("bq2", [P, NC])
        bk2 = sb("bk2", [P, NC])
        bm1 = sb("bm1", [P, 2 * HID // P])
        bm1_half = sb("bm1_half", [P, HID // P])
        hid_bias = sb("hid_bias", [P, B, 2 * NCH])
        rout_bias = sb("rout_bias", [E, B])
        ada = sb("ada", [P, B, 6 * NC])
        head_mask = sb("head_mask", [P, HPT])

        minus_half = sb("minus_half", [P, NT, 1])

        x_in = sb("x_in", [P, NT, C])
        x_res = sb("x_res", [P, NT, C])
        ctx_in = sb("ctx_in", [P, NT, C])
        wso_gated = sb("wso_gated", [P, NC, C])
        wco_gated = sb("wco_gated", [P, NC, C])
        grow = sb("grow", [P, 6, C])

        WORK_COLS = 23400
        work = sb("work", [P, WORK_COLS])

        def carver():
            at = [0]

            def carve(*dims):
                n = 1
                for d in dims:
                    n *= d
                a, at[0] = at[0], at[0] + n
                assert at[0] <= WORK_COLS, at
                v = work[:, a:a + n]
                if len(dims) == 2:
                    v = v.rearrange("p (a b) -> p a b", a=dims[0])
                if len(dims) == 3:
                    v = v.rearrange("p (a b c) -> p a b c", a=dims[0], b=dims[1])
                return v
            return carve

        room = carver()
        ctxT = room(NC, T)
        nx = room(NT, C)
        p0 = nx
        nxT = room(NC, T)
        kpT = room(NC, T)
        pT0 = room(NT, T)
        evT = room(NC, T)
        th = room(4, T)
        hid = room(NCH, T)
        zg = room(NT, C)
        acc = room(NT, C)
        x1 = room(NT, C)
        xn = room(NT, C)
        hT = room(NC, T)
        oT = hT
        qT = room(NC, T)
        kT1 = room(NC, T)
        kT2 = room(NC, T)
        KM = room(H, T)
        gated = KM[:, 0:HID // P, :]
        thm = KM[:, HID // P:HID // P + 4, :]
        va1 = room(NT, H, VA)
        va2 = room(NT, H, VA)
        es = room(3, 512)
        et = room(2, 512)
        s1 = room(512)
        s2 = room(2, 512)
        o = room(NT, C)
        xb = room(NT, C)
        tmp = room(NT, C)
        xs = room(NT, C)

        hb = sb("hb", [P, 2 * NCH])
        rb = sb("rb", [E, 1])
        ad = sb("ad", [P, 6 * NC])
        st0 = sb("st0", [P, NT, 6])
        mv0 = sb("mv0", [P, NT, 2])
        rstd0 = sb("rstd0", [P, NT, 1])
        st1 = sb("st1", [P, NT, 6])
        mv1 = sb("mv1", [P, NT, 2])
        rstd1 = sb("rstd1", [P, NT, 1])
        nm0 = sb("nm0", [P, NT])
        sum0 = sb("sum0", [P, NT])
        r0 = sb("r0", [P, NT])
        lgT = sb("lgT", [E, T])
        lmax = sb("lmax", [P, NT, 1])
        lsub = sb("lsub", [P, NT, E])
        lexp = sb("lexp", [P, NT, E])
        lsum = sb("lsum", [P, NT, 1])
        lrec = sb("lrec", [P, NT, 1])
        prob = sb("prob", [P, NT, E])
        nms = sb("nms", [P, 2, 4])
        m8 = sb("m8", [P, 2, 4, 8])
        nmc = sb("nmc", [P, 2, 2])
        ro = sb("ro", [P, NT, H, 1])

        weights_loaded = sem("weights_loaded")
        square_loaded = sem("square_weights_loaded")
        w2_loaded = sem("e_w2_loaded")
        evidence_loaded = sem("evidence_rows_loaded")
        anchor_loaded = sem("anchor_rows_loaded")
        ada_loaded = sem("ada_loaded")
        pool_setup = sem("pool_setup")
        ident_ready = sem("ident_ready")
        cond_tanh_ready = sem("cond_tanh_ready")
        scond_ready = sem("scond_ready")
        setup_mm = sem("setup_mm")
        setup_ev = sem("setup_ev")
        rows_ready = sem("gate_rows_ready")
        rows_stored = sem("gate_rows_stored")
        setup_done = sem("setup_done")
        ones_ready = sem("ones_ready")
        x_loaded = signal("x_loaded", 48)
        ctx_loaded = signal("ctx_loaded", 16)
        grow_loaded = signal("gate_rows_loaded", 16)
        x_copied = signal("x_copied", 1)
        stored = signal("stored", 48)
        stats0 = signal("layer0_stats", 4)
        rstd0_ready = signal("layer0_rstd_ready", 2)
        nx_ready = signal("nx_ready", 2)
        hb_ready = signal("hidden_bias_ready", 1)
        rb_ready = signal("router_bias_ready", 1)
        ctxT_ready = signal("ctxT_ready", 1)
        nxT_ready = signal("nxT_ready", 2)
        kp_ready = signal("kp_ready", 1)
        nm0_ready = signal("layer0_max_ready", 1)
        exp0_ready = signal("layer0_exp_ready", 2)
        r0_ready = signal("layer0_recip_ready", 1)
        p0_ready = signal("layer0_weights_ready", 2)
        pT0_ready = signal("layer0_weightsT_ready", 1)
        evT_ready = signal("evT_ready", 1)
        lgT_ready = signal("logitsT_ready", 1)
        router = signal("router_vector", 5)
        lexp_ready = signal("router_exp_ready", 1)
        tanh0 = signal("layer0_tanh", NCH)
        biased0 = signal("layer0_biased", NCH)
        times0 = signal("layer0_tanh_times_biased", NCH)
        hid_ready = signal("layer0_hidden_ready", NCH)
        mix = signal("experts_mixed", 12)
        zg_ready = signal("gate_sum_ready", 1)
        tg_ready = signal("gate_tanh_ready", 1)
        x1_ready = signal("x1_ready", 2)
        ad_ready = signal("ada_ready", 1)
        stats1 = signal("layer1_stats", 12)
        rstd1_ready = signal("layer1_rstd_ready", 6)
        xn_ready = signal("xn_ready", 6)
        hT_ready = signal("hT_ready", 6)
        q_ready = signal("q_ready", 4)
        k1_ready = signal("k1_ready", 2)
        k2_ready = signal("k2_ready", 2)
        va1_ready = signal("v1_ready", 2)
        va2_ready = signal("v2_ready", 2)
        km1a_ready = signal("self_masked_keys_ready", HPT)
        km1b_ready = signal("self_masked_keys_of_gpsimd_ready", HPT // 2)
        km2_ready = signal("cross_masked_keys_ready", H // 2)
        max1_ready = signal("self_max_ready", SELF_GROUPS)
        exp1_ready = signal("self_exp_ready", 4 * SELF_GROUPS)
        et1_ready = signal("self_weightsT_ready", SELF_GROUPS)
        top = signal("top16_vector", 9 * CROSS_GROUPS)
        exp2_ready = signal("cross_exp_ready", 2 * CROSS_GROUPS)
        rest_ready = signal("cross_exp_of_the_rest_ready", 2 * CROSS_GROUPS)
        p2_ready = signal("cross_weights_ready", CROSS_GROUPS)
        et2_ready = signal("cross_weightsT_ready", CROSS_GROUPS)
        ro_ready = signal("heads_recip_ready", 4)
        o_ready = signal("heads_ready", 4)
        oT_ready = signal("headsT_ready", 2)
        xb_ready = signal("residual_plus_bias_ready", 3)
        gy_ready = signal("gated_out_ready", 1)
        wgated_ready = signal("gated_weights_ready", 2)
        xs_ready = signal("residual_ready", 3)
        tanh1 = signal("mlp_tanh", 8)
        silu1 = signal("mlp_silu_ready", 8)
        biased1 = signal("mlp_biased", 8)
        gated_ready = signal("mlp_gated", 8)

        banks = [ctx.enter_context(nc.psum_tensor(f"bank{i}", [P, 512], F32)) for i in range(8)]
        L0 = Products([("ctxT", 0, 1), ("nxT", 1, 1), ("kp", 0, 1), ("sc", 1, 1), ("PT", 0, 1), ("evT", 1, 1),
                       ("lgT", 0, 1), ("lg", 1, 1)] + [(f"h{n}", n % 2, 1) for n in range(NCH)]
                      + [("g", 0, 1)] + [(f"y{n}", 1 - n % 2, 1) for n in range(E * NT)],
                      banks[0:2], [sem(f"bank{i}_layer0_written") for i in range(2)])
        plan1 = [("k2", 2, 1), ("v2", 3, 1), ("hT1", 7, 1), ("q1", 2, 1), ("k1", 3, 1), ("v1", 5, 1)]
        for g in range(SELF_GROUPS):
            plan1 += [(("S1", g), 2 + g % 2, 1), (("T1", g), 4 + g % 2, 1)]
        plan1 += [(("O1", w), 6 + w, 4) for w in range(2)]
        plan1 += [("oT1", 4, 1), ("so", 5, 1), ("hT2", 4, 1), ("q2", 5, 1)]
        for g in range(CROSS_GROUPS):
            plan1 += [(("S2", g), 2 + g % 2, 1), (("T2", g), 4 + g % 2, 1)]
        plan1 += [(("O2", t), 6 + t, 8) for t in range(NT)]
        plan1 += [("oT2", 4, 1), ("co", 5, 1)]
        L1 = Products(plan1, banks, [sem(f"bank{i}_attention_written") for i in range(8)])
        LM = Products([("hT3", 4, 1)] + [(("m", j), (2, 3, 5, 4)[j % 4], 1) for j in range(HID // P)] + [("y", 6, 1)],
                      banks, [sem(f"bank{i}_mlp_written") for i in range(8)])

        gate_rows = nc.dram_tensor("gate_rows", (B, 6, C), F32, kind="Internal").ap()

        raw = carver()
        raw_q, raw_k, raw_v, raw_o = [raw(NC, C) for _ in range(4)]
        tq, tk, tv = [raw(NC, C) for _ in range(3)]
        tw2 = raw(NC, EXP_COLS)
        raw_ev = raw(NC, W1_COLS)
        raw_an = raw(NC, W1_COLS)
        raw_ada = raw(NC, 9 * C)
        cond_col = raw(NC, B)
        cond_tanh = raw(NC, B)
        scond = raw(NC, B)
        hid_b = raw(NCH)
        ada_b = raw(6 * NC)
        rout_b = raw(1)
        eb2_col = raw(NC, E, 1)
        eb2_cols = raw(NC, E, P)
        bv_col = raw(NC, 2, 1)
        bv_cols = raw(NC, 2, B)
        gate_bias = raw(3, C)
        row_bias = raw(3, C)
        mrow = raw(6, C)

        def col(v):
            return v.rearrange("(c p) -> p c", p=P)

        def rows(v):
            return v.rearrange("(c p) n -> p c n", p=P)

        def row(v, n):
            return v.partition_broadcast(n)

        square_loads = [(raw_q, rows(Wq)), (raw_k, rows(Wk)), (raw_v, rows(Wv)), (raw_o, rows(out_w))]
        w2_loads = [(w2[:, 4 * e:4 * e + 4, :], rows(e_w2[e])) for e in range(E)]
        evidence_loads = [(raw_ev[:, :, e * RH:(e + 1) * RH], rows(e_w1[e, C:2 * C, :])) for e in range(E)]
        evidence_loads += [(raw_ev[:, :, GATE_COL:ROUT_COL], rows(gate_w1[C:2 * C, :])),
                           (raw_ev[:, :, ROUT_COL:W1_COLS], rows(router_W[C:2 * C, :]))]
        anchor_loads = [(cond_col[:, c, :], cond_1024[:, c * P:(c + 1) * P].rearrange("b p -> p b")) for c in range(NC)]
        anchor_loads += [(raw_an[:, :, e * RH:(e + 1) * RH], rows(e_w1[e, 2 * C:3 * C, :])) for e in range(E)]
        anchor_loads += [(raw_an[:, :, GATE_COL:ROUT_COL], rows(gate_w1[2 * C:3 * C, :])),
                         (raw_an[:, :, ROUT_COL:W1_COLS], rows(router_W[2 * C:3 * C, :])),
                         (hid_b[:, 12:14], col(gate_b1)), (rout_b[0:E, :], router_b.rearrange("(e a) -> e a", a=1)),
                         (bv_col[:, :, 0, 0], col(b_qkv[2 * C:3 * C])), (bv_col[:, :, 1, 0], col(b_kv[C:2 * C]))]
        ada_loads = [(raw_ada, rows(w_ada))]
        for e in range(E):
            anchor_loads += [(hid_b[:, 4 * e:4 * e + 4], col(e_b1[e])), (eb2_col[:, :, e, 0], col(e_b2[e]))]
            ada_loads += [(ada_b[:, 4 * e:4 * e + 4], col(b_ada[3 * e * C:(3 * e + 2) * C])),
                          (gate_bias[0:B, e, :], row(b_ada[(3 * e + 2) * C:(3 * e + 3) * C], B))]
        ada_loads += [(row_bias[0:B, s, :], row(v, B)) for s, v in enumerate((b_so, b_co, b_m2))]
        weight_loads = [
            (w1[:, 0:NC, GATE_COL:ROUT_COL], rows(gate_w1[0:C, :])),
            (w1[:, 0:NC, ROUT_COL:W1_COLS], rows(router_W[0:C, :])),
            (wg2[:, :, :], rows(gate_w2)), (wqkv[:, :, :], rows(w_qkv)), (wso[:, :, :], rows(w_so)),
            (wq2[:, :, :], rows(w_q)), (wkv[:, :, :], rows(w_kv)), (wco[:, :, :], rows(w_co)),
            (wm1[:, :, :], rows(w_m1)), (wm2[:, :, :], rows(w_m2)),
            (gamma[:, :], col(ln_gamma)), (beta[:, :], col(ln_beta)),
            (gate_b2_all[:, 0, :], row(gate_b2, P)), (out_b_all[:, :], row(out_b, P)),
            (bq1[:, :], col(b_qkv[0:C])), (bk1[:, :], col(b_qkv[C:2 * C])),
            (bq2[:, :], col(b_q)), (bk2[:, :], col(b_kv[0:C])), (bm1[:, :], col(b_m1)),
        ] + [(w1[:, 0:NC, e * RH:(e + 1) * RH], rows(e_w1[e, 0:C, :])) for e in range(E)]
        SQUARE_LOADED, W2_LOADED, EVIDENCE_LOADED, ANCHOR_LOADED, ADA_LOADED, WEIGHTS_LOADED = [
            16 * len(loads) for loads in (square_loads, w2_loads, evidence_loads, anchor_loads, ada_loads, weight_loads)]

        SETUP = ([("tq", c) for c in range(NC)] + [("tk", c) for c in range(NC)] + [("tv", c) for c in range(NC)]
                 + [("tw2", k) for k in range(6)] + [("wqk", c) for c in range(NC)] + [("w2", k) for k in range(6)]
                 + [("ev", c, n) for c in range(NC) for n in range(0, W1_COLS, 512)]
                 + [("eb2", e) for e in range(E)]
                 + [("hid",), ("rout",), ("ada",)] + [("gate", s) for s in range(3)] + [("bias", s) for s in range(2)])

        block = ctx.enter_context(nc.Block())

        @block.sync
        def _(sp):
            with nc.allow_non_contiguous_dma(reason="vectors down the partitions, once"):
                for dst, src in square_loads:
                    sp.dma_start(dst, src).then_inc(square_loaded, 16)
                for dst, src in w2_loads:
                    sp.dma_start(dst, src).then_inc(w2_loaded, 16)
                for dst, src in evidence_loads:
                    sp.dma_start(dst, src).then_inc(evidence_loaded, 16)
                for dst, src in anchor_loads:
                    sp.dma_start(dst, src).then_inc(anchor_loaded, 16)
                for dst, src in ada_loads:
                    sp.dma_start(dst, src).then_inc(ada_loaded, 16)
                for dst, src in weight_loads:
                    sp.dma_start(dst, src).then_inc(weights_loaded, 16)

            def load_ctx(b):
                if later(b):
                    sp.wait_ge(L0.sem("evT"), L0.at(b - 1, "evT"))
                    sp.wait_ge(L0.sem("ctxT"), L0.at(b - 1, "ctxT"))
                sp.dma_start(ctx_in[:, :, :], ctx_1024[bass.ds(b, 1), :, :].rearrange("a (t p) c -> p (a t) c", p=P))\
                    .then_inc(ctx_loaded.sem, 16)

            def load_x(b):
                if later(b):
                    sp.wait_ge(x_copied.sem, x_copied.at(b - 1))
                    sp.wait_ge(nx_ready.sem, nx_ready.at(b - 1))
                for dst, lo in ((x_in[:, 0, :], SHIFT), (x_in[0:P - SHIFT, 1, :], SHIFT + P), (x_in[P - SHIFT:P, 1, :], 0)):
                    n = dst.shape[0]
                    sp.dma_start(dst, x[bass.ds(b, 1), lo:lo + n, :].rearrange("a p c -> (a p) c")).then_inc(x_loaded.sem, 16)

            def load_rows(b):
                if later(b):
                    sp.wait_ge(gy_ready.sem, gy_ready.at(b - 1))
                    sp.wait_ge(xb_ready.sem, xb_ready.at(b - 1))
                sp.dma_start(grow[:, :, :].rearrange("p s c -> p (s c)"),
                             gate_rows[bass.ds(b, 1), :, :].rearrange("a s c -> (a s c)").partition_broadcast(P))\
                    .then_inc(grow_loaded.sem, 16)

            def store(b):
                sp.wait_ge(xs_ready.sem, xs_ready.at(b))
                for src, lo in ((xs[:, 0, :], SHIFT), (xs[0:P - SHIFT, 1, :], SHIFT + P), (xs[P - SHIFT:P, 1, :], 0)):
                    n = src.shape[0]
                    sp.dma_start(out[bass.ds(b, 1), lo:lo + n, :].rearrange("a p c -> (a p) c"), src).then_inc(stored.sem, 16)

            load_x(0)
            load_ctx(0)
            sp.wait_ge(rows_ready, 1)
            sp.dma_start(gate_rows[:, :, :], mrow[0:B, :, :]).then_inc(rows_stored, 16)
            sp.wait_ge(rows_stored, 16)
            load_rows(0)
            load_x(1)
            load_ctx(1)
            load_x(2)
            load_ctx(2)
            with sp.Fori(2, B - 1) as i:
                store(i - 2)
                load_rows(i - 1)
                load_x(i + 1)
                load_ctx(i + 1)
            for b in (B - 3, B - 2):
                store(b)
                load_rows(b + 1)
            store(B - 1)
            sp.wait_ge(stored.sem, stored.at(B - 1))

        @block.gpsimd
        def _(pool):
            g = nc.gpsimd
            g.memset(ident[:, :], 0.0).then_inc(pool_setup, 1)
            pool.wait_ge(pool_setup, 1)
            g.affine_select(out=ident[:, :], in_=ident[:, :], compare_op=ALU.not_equal, fill=1.0,
                            base=0, pattern=[[-1, P]], channel_multiplier=1).then_inc(ident_ready, 1)
            g.memset(head_mask[:, :], 1.0).then_inc(pool_setup, 1)
            pool.wait_ge(pool_setup, 2)
            g.affine_select(out=head_mask[:, :], in_=head_mask[:, :], compare_op=ALU.is_ge, fill=0.0,
                            base=0, pattern=[[-D, HPT]], channel_multiplier=1).then_inc(pool_setup, 1)
            pool.wait_ge(pool_setup, 3)
            g.affine_select(out=head_mask[:, :], in_=head_mask[:, :], compare_op=ALU.is_ge, fill=0.0,
                            base=D - 1, pattern=[[D, HPT]], channel_multiplier=-1).then_inc(pool_setup, 1)
            pool.wait_ge(setup_done, 1)
            pool.wait_ge(rows_stored, 16)
            g.memset(va1[:, :, :, D:VA], 1.0).then_inc(ones_ready, 1)
            g.memset(va2[:, :, :, D:VA], 1.0).then_inc(ones_ready, 1)
            g.memset(minus_half[:, :, :], -0.5).then_inc(pool_setup, 1)
            pool.wait_ge(pool_setup, 5)

            def alone():
                pool.nop(nofuse=True)

            def fill(slot, a):
                for name in FILL.get(slot, []) if a is not None else []:
                    if name == "nx":
                        inverse_deviation(a, 0, rstd0, rstd0_ready)
                        pool.wait_ge(x_loaded.sem, x_loaded.at(a))
                        if later(a):
                            pool.wait_ge(x1_ready.sem, x1_ready.at(a - 1))
                        alone()
                        g.tensor_copy(x_res[:, :, :], x_in[:, :, :]).then_inc(x_copied.sem, 1)
                    if name[0] == "h":
                        n = int(name[1:])
                        pool.wait_ge(tanh0.sem, tanh0.at(a, n + 1))
                        pool.wait_ge(biased0.sem, biased0.at(a, n + 1))
                        g.tensor_tensor(th[:, n % 4, :], th[:, n % 4, :], hid[:, n, :], ALU.mult).then_inc(times0.sem, 1)
                        pool.wait_ge(times0.sem, times0.at(a, n + 1))
                        g.tensor_tensor(hid[:, n, :], th[:, n % 4, :], hid[:, n, :], ALU.add).then_inc(hid_ready.sem, 1)

            def masked_keys(src, first, ready):
                for h in range(first, H, 2):
                    m = h % HPT
                    g.tensor_tensor(KM[:, h:h + 2, :], src[:, h // HPT:h // HPT + 1, :].broadcast_to([P, 2, T]),
                                    head_mask[:, m:m + 2].unsqueeze(2).broadcast_to([P, 2, T]), ALU.mult).then_inc(ready.sem, 1)

            def inverse_deviation(b, n, dst, ready):
                pool.wait_ge(ready.sem, ready.at(b, 2 * n + 1))
                g.tensor_tensor(dst[:, :, :], dst[:, :, :], minus_half[:, :, :], ALU.pow).then_inc(ready.sem, 1)

            def gated_weights(b, s, w, dst):
                if s == 0:
                    pool.wait_ge(grow_loaded.sem, grow_loaded.at(b))
                    if later(b):
                        pool.wait_ge(gy_ready.sem, gy_ready.at(b - 1))
                g.tensor_tensor(dst[:, :, :], w[:, :, :], grow[:, 2 * s:2 * s + 1, :].broadcast_to([P, NC, C]), ALU.mult)\
                    .then_inc(wgated_ready.sem, 1)

            def plus_bias(b, s, src):
                if s:
                    pool.wait_ge(xs_ready.sem, xs_ready.at(b, s))
                else:
                    pool.wait_ge(grow_loaded.sem, grow_loaded.at(b))
                    pool.wait_ge(x1_ready.sem, x1_ready.at(b))
                    if later(b):
                        pool.wait_ge(xs_ready.sem, xs_ready.at(b - 1))
                g.tensor_tensor(xb[:, :, :], src[:, :, :], grow[:, 2 * s + 1:2 * s + 2, :].broadcast_to([P, NT, C]), ALU.add)\
                    .then_inc(xb_ready.sem, 1)

            def iteration(a, b, c):
                fill("norm3", a)
                for j in range(HID // P):
                    fill(("mlp", j), a)
                    if j == NORM1_STEP and b is not None:
                        inverse_deviation(b, 0, rstd1, rstd1_ready)
                fill("silu", a)
                fill("proj1", a)
                if b is not None:
                    if later(b):
                        pool.wait_ge(gy_ready.sem, gy_ready.at(b - 1))
                    pool.wait_ge(k1_ready.sem, k1_ready.at(b))
                    alone()
                    masked_keys(kT1, HPT, km1b_ready)
                    plus_bias(b, 0, x1)
                    gated_weights(b, 0, wso, wso_gated)
                    gated_weights(b, 1, wco, wco_gated)
                fill("keys1", a)
                for s in range(SELF_GROUPS + PV_LAG):
                    fill(("self", s), a)
                if b is not None:
                    for s in (SELF_GROUPS - 2, SELF_GROUPS - 1):
                        pool.wait_ge(L1.sem(("S1", s)), L1.at(b, ("S1", s)))
                    pool.wait_ge(k2_ready.sem, k2_ready.at(b))
                    pool.wait_ge(km1a_ready.sem, km1a_ready.at(b))
                    alone()
                    masked_keys(kT2, 0, km2_ready)
                fill("heads1", a)
                fill("out1", a)
                if b is not None:
                    inverse_deviation(b, 1, rstd1, rstd1_ready)
                    plus_bias(b, 1, xs)
                fill("norm2", a)
                fill("proj2", a)
                fill("keys2", a)
                for s in range(CROSS_GROUPS + PV_LAG):
                    if b is not None and s < CROSS_GROUPS:
                        pool.wait_ge(exp2_ready.sem, exp2_ready.at(b, 2 * s + 2))
                        pool.wait_ge(rest_ready.sem, rest_ready.at(b, 2 * s + 2))
                        g.tensor_tensor(es[:, s % 3, :], es[:, s % 3, :], s2[:, s % 2, :], ALU.subtract).then_inc(p2_ready.sem, 1)
                    fill(("cross", s), a)
                fill("heads2", a)
                fill("out2", a)
                if b is not None:
                    inverse_deviation(b, 2, rstd1, rstd1_ready)
                    plus_bias(b, 2, xs)
                fill("end", a)

            iteration(0, None, None)
            iteration(1, 0, None)
            with pool.Fori(2, B) as i:
                iteration(i, i - 1, i - 2)
            iteration(None, B - 1, B - 2)
            iteration(None, None, B - 1)

        @block.scalar
        def _(act):
            A = nc.scalar.activation
            act.wait_ge(anchor_loaded, ANCHOR_LOADED)
            A(cond_tanh[:, :, :], cond_col[:, :, :], ACT.Tanh, scale=0.5).then_inc(cond_tanh_ready, 1)
            act.wait_ge(setup_done, 1)

            def transposed(b, products, name, dst, signal_):
                act.wait_ge(products.sem(name), products.at(b, name))
                A(dst, products.bank(name)[:, :].rearrange("p (a n) -> p a n", a=2), ACT.Copy).then_inc(signal_.sem, 1)

            def fill(slot, a):
                for name in FILL.get(slot, []) if a is not None else []:
                    if name == "ctxT":
                        transposed(a, L0, name, ctxT[:, :, :], ctxT_ready)
                        if later(a):
                            act.wait_ge(lgT_ready.sem, lgT_ready.at(a - 1))
                        A(rb[:, :], rout_bias[:, bass.ds(a, 1)], ACT.Copy).then_inc(rb_ready.sem, 1)
                    if name == "nxT":
                        act.wait_ge(L0.sem(name), L0.at(a, name))
                        for c in range(NC):
                            A(nxT[:, c, :], L0.bank(name)[:, c * T:(c + 1) * T], ACT.Identity,
                              bias=beta[:, c:c + 1], scale=gamma[:, c:c + 1]).then_inc(nxT_ready.sem, 1)
                    if name == "sc":
                        act.wait_ge(nm0_ready.sem, nm0_ready.at(a))
                        for t in range(NT):
                            A(p0[:, t, :], L0.bank(name)[:, t * T:(t + 1) * T], ACT.Exp, bias=nm0[:, t:t + 1],
                              accum_out=sum0[:, t:t + 1]).then_inc(exp0_ready.sem, 1)
                    if name == "PT":
                        transposed(a, L0, name, pT0[:, :, :], pT0_ready)
                    if name == "lgT":
                        act.wait_ge(L0.sem(name), L0.at(a, name))
                        act.wait_ge(rb_ready.sem, rb_ready.at(a))
                        A(lgT[:, :], L0.bank(name)[0:E, 0:T], ACT.Identity, bias=rb[:, :]).then_inc(lgT_ready.sem, 1)
                    if name == "lg":
                        act.wait_ge(router.sem, router.at(a, 2))
                        A(lexp[:, :, :], lsub[:, :, :], ACT.Exp).then_inc(lexp_ready.sem, 1)
                    if name[0] == "h":
                        n = int(name[1:])
                        act.wait_ge(L0.sem(name), L0.at(a, name))
                        if n == 0:
                            act.wait_ge(hb_ready.sem, hb_ready.at(a))
                        if n == 0 and later(a):
                            act.wait_ge(L0.sem("y4"), L0.at(a - 1, "y4"))
                            act.wait_ge(L0.sem("y5"), L0.at(a - 1, "y5"))
                        if n >= 4:
                            act.wait_ge(hid_ready.sem, hid_ready.at(a, n - 3))
                        elif n == 0 and later(a):
                            act.wait_ge(hid_ready.sem, hid_ready.at(a - 1))
                        A(th[:, n % 4, :], L0.bank(name)[:, 0:T], ACT.Tanh, bias=hb[:, NCH + n:NCH + n + 1], scale=0.5)\
                            .then_inc(tanh0.sem, 1)
                        A(hid[:, n, :], L0.bank(name)[:, 0:T], ACT.Identity, bias=hb[:, n:n + 1]).then_inc(biased0.sem, 1)
                    if name == "g":
                        act.wait_ge(zg_ready.sem, zg_ready.at(a))
                        A(zg[:, :, :], zg[:, :, :], ACT.Tanh, scale=0.5).then_inc(tg_ready.sem, 1)

            def normed(b, n, products):
                name = f"hT{n + 1}"
                act.wait_ge(products.sem(name), products.at(b, name))
                act.wait_ge(ad_ready.sem, ad_ready.at(b))
                for c in range(NC):
                    A(hT[:, c, :], products.bank(name)[:, c * T:(c + 1) * T], ACT.Identity,
                      bias=ad[:, 4 * n + c:4 * n + c + 1], scale=ad[:, 4 * n + 2 + c:4 * n + 3 + c]).then_inc(hT_ready.sem, 1)

            def queries(b, name, bias):
                act.wait_ge(L1.sem(name), L1.at(b, name))
                for c in range(NC):
                    A(qT[:, c, :], L1.bank(name)[:, c * T:(c + 1) * T], ACT.Identity,
                      bias=bias[:, c:c + 1], scale=0.25).then_inc(q_ready.sem, 1)

            def weightsT(b, kind, g, et_ready, o_name, part):
                act.wait_ge(L1.sem((kind, g)), L1.at(b, (kind, g)))
                if g >= 2:
                    act.wait_ge(L1.sem(o_name), L1.at(b, o_name, part))
                A(et[:, g % 2, :], L1.bank((kind, g))[:, :], ACT.Copy).then_inc(et_ready.sem, 1)

            def iteration(a, b, c):
                if c is not None:
                    normed(c, 2, LM)
                if b is not None:
                    act.wait_ge(L1.sem("k2"), L1.at(b, "k2"))
                    if later(b):
                        act.wait_ge(km2_ready.sem, km2_ready.at(b - 1))
                    for t in range(NC):
                        A(kT2[:, t, :], L1.bank("k2")[:, t * T:(t + 1) * T], ACT.Identity, bias=bk2[:, t:t + 1])\
                            .then_inc(k2_ready.sem, 1)
                fill("norm3", a)
                for j in range(HID // P):
                    if c is not None:
                        act.wait_ge(LM.sem(("m", j)), LM.at(c, ("m", j)))
                        if j >= 4:
                            act.wait_ge(silu1.sem, silu1.at(c, j - 3))
                        A(thm[:, j % 4, :], LM.bank(("m", j))[:, 0:T], ACT.Tanh, bias=bm1_half[:, j:j + 1], scale=0.5)\
                            .then_inc(tanh1.sem, 1)
                        A(gated[:, j, :], LM.bank(("m", j))[:, 0:T], ACT.Identity, bias=bm1[:, j:j + 1]).then_inc(biased1.sem, 1)
                    fill(("mlp", j), a)
                if b is not None:
                    normed(b, 0, L1)
                fill("silu", a)
                fill("proj1", a)
                if b is not None:
                    queries(b, "q1", bq1)
                fill("keys1", a)
                for s in range(SELF_GROUPS + PV_LAG):
                    if b is not None and s < SELF_GROUPS:
                        act.wait_ge(max1_ready.sem, max1_ready.at(b, s + 1))
                        if s >= 3:
                            act.wait_ge(L1.sem(("T1", s - 3)), L1.at(b, ("T1", s - 3)))
                        for u in range(4):
                            A(es[:, s % 3, u * P:(u + 1) * P], L1.bank(("S1", s))[:, u * P:(u + 1) * P], ACT.Exp,
                              bias=nms[:, s % 2, u:u + 1]).then_inc(exp1_ready.sem, 1)
                    fill(("self", s), a)
                    g = s - S_LAG
                    if b is not None and 0 <= g < SELF_GROUPS:
                        weightsT(b, "T1", g, et1_ready, ("O1", (g - 2) // 4), (g - 2) % 4 + 1)
                fill("heads1", a)
                if b is not None:
                    transposed(b, L1, "oT1", oT[:, :, :], oT_ready)
                fill("out1", a)
                fill("norm2", a)
                if b is not None:
                    normed(b, 1, L1)
                fill("proj2", a)
                if b is not None:
                    queries(b, "q2", bq2)
                fill("keys2", a)
                for s in range(CROSS_GROUPS + PV_LAG):
                    if b is not None and s < CROSS_GROUPS:
                        act.wait_ge(top.sem, top.at(b, 9 * s + 5))
                        if s >= 3:
                            act.wait_ge(L1.sem(("T2", s - 3)), L1.at(b, ("T2", s - 3)))
                        for u in range(2):
                            A(es[:, s % 3, u * T:(u + 1) * T], L1.bank(("S2", s))[:, u * T:(u + 1) * T], ACT.Exp,
                              bias=nmc[:, s % 2, u:u + 1]).then_inc(exp2_ready.sem, 1)
                        for u in range(2):
                            act.wait_ge(top.sem, top.at(b, 9 * s + 8 + u))
                            A(s2[:, s % 2, u * T:(u + 1) * T], s2[:, s % 2, u * T:(u + 1) * T], ACT.Exp,
                              bias=nmc[:, s % 2, u:u + 1]).then_inc(rest_ready.sem, 1)
                    fill(("cross", s), a)
                    g = s - S_LAG
                    if b is not None and 0 <= g < CROSS_GROUPS:
                        weightsT(b, "T2", g, et2_ready, ("O2", (g - 2) // 8), (g - 2) % 8 + 1)
                fill("heads2", a)
                if b is not None:
                    transposed(b, L1, "oT2", oT[:, :, :], oT_ready)
                fill("out2", a)
                fill("end", a)

            iteration(0, None, None)
            iteration(1, 0, None)
            with act.Fori(2, B) as i:
                iteration(i, i - 1, i - 2)
            iteration(None, B - 1, B - 2)
            iteration(None, None, B - 1)

        @block.vector
        def _(dve):
            v = nc.vector

            def alone():
                dve.nop(nofuse=True)

            done = [0]

            def step(ins):
                done[0] += 1
                ins.then_inc(setup_ev, 1)

            for i, p in enumerate(SETUP):
                bank, kind = banks[i % 8], p[0]
                if p == ("eb2", 0):
                    dve.wait_ge(cond_tanh_ready, 1)
                    v.scalar_tensor_tensor(scond[:, :, :], cond_tanh[:, :, :], 1.0, cond_col[:, :, :], ALU.add, ALU.mult)\
                        .then_inc(scond_ready, 1)
                    dve.wait_ge(scond_ready, 1)
                    v.tensor_scalar(scond[:, :, :], scond[:, :, :], 0.5, None, ALU.mult).then_inc(scond_ready, 1)
                    v.tensor_copy(eb2_cols[:, :, :, :], eb2_col[:, :, :, :].broadcast_to([P, NC, E, P])).then_inc(scond_ready, 1)
                    v.tensor_copy(bv_cols[:, :, :, :], bv_col[:, :, :, :].broadcast_to([P, NC, 2, B])).then_inc(scond_ready, 1)
                dve.wait_ge(setup_mm, i + 1)
                if kind in ("tq", "tk", "tv"):
                    dst = {"tq": tq, "tk": tk, "tv": tv}[kind]
                    step(v.tensor_copy(dst[:, p[1], :], bank[:, 0:C]))
                elif kind == "tw2":
                    step(v.tensor_copy(tw2[:, :, 2 * P * p[1]:2 * P * (p[1] + 1)], bank[:, :].rearrange("p (c n) -> p c n", c=NC)))
                elif kind == "wqk":
                    step(v.tensor_scalar(wqk[:, p[1], :], bank[:, 0:C], float(C) ** -0.5, None, ALU.mult))
                elif kind == "ev":
                    n = min(512, W1_COLS - p[2])
                    step(v.tensor_copy(w1[:, NC + p[1], p[2]:p[2] + n], bank[:, 0:n]))
                elif kind == "w2":
                    step(v.tensor_scalar(w2[:, 2 * p[1]:2 * p[1] + 2, :], bank[:, :].rearrange("p (k n) -> p k n", k=2), 0.25, None, ALU.mult))
                elif kind == "eb2":
                    step(v.tensor_scalar(e_b2_all[:, p[1], :], bank[:, 0:C], 0.5, None, ALU.mult))
                elif kind == "hid":
                    dve.wait_ge(anchor_loaded, ANCHOR_LOADED)
                    step(v.tensor_tensor(hid_bias[:, :, 0:NCH].rearrange("p b j -> p j b"),
                                         bank[:, 0:NCH * B].rearrange("p (j b) -> p j b", j=NCH),
                                         hid_b.unsqueeze(2).broadcast_to([P, NCH, B]), ALU.add))
                elif kind == "rout":
                    step(v.tensor_scalar(rout_bias[:, :], bank[0:E, 0:B], rout_b[0:E, :], None, ALU.add))
                elif kind == "ada":
                    dve.wait_ge(ada_loaded, ADA_LOADED)
                    step(v.tensor_tensor(ada[:, :, :].rearrange("p b j -> p j b"),
                                         bank[:, 0:6 * NC * B].rearrange("p (j b) -> p j b", j=6 * NC),
                                         ada_b.unsqueeze(2).broadcast_to([P, 6 * NC, B]), ALU.add))
                elif kind == "gate":
                    step(v.tensor_tensor(mrow[0:B, 2 * p[1], :], bank[0:B, 0:C], gate_bias[0:B, p[1], :], ALU.add))
                elif kind == "bias":
                    step(v.tensor_tensor(row_bias[0:B, p[1], :], bank[0:B, 0:C], row_bias[0:B, p[1], :], ALU.add))
            dve.wait_ge(setup_ev, len(SETUP))
            dve.wait_ge(weights_loaded, WEIGHTS_LOADED)
            v.tensor_tensor(mrow[0:B, 1:6:2, :], row_bias[0:B, :, :], mrow[0:B, 0:6:2, :], ALU.mult).then_inc(rows_ready, 1)
            v.tensor_scalar(hid_bias[:, :, NCH:], hid_bias[:, :, 0:NCH], 0.5, None, ALU.mult).then_inc(scond_ready, 1)
            for n in range(3):
                w = ada[:, :, 4 * n + 2:4 * n + 4]
                v.tensor_scalar(w, w, 1.0, None, ALU.add).then_inc(scond_ready, 1)
            for w, s in ((wg2[:, :, :], 0.5), (wm2[:, :, :], 0.5), (out_b_all[:, :], 0.5), (bq1[:, :], 0.25), (bq2[:, :], 0.25)):
                v.tensor_scalar(w, w, s, None, ALU.mult).then_inc(scond_ready, 1)
            v.tensor_scalar(bm1_half[:, :], bm1[:, 0:HID // P], 0.5, None, ALU.mult).then_inc(scond_ready, 1)
            dve.wait_ge(scond_ready, 14)
            dve.wait_ge(rows_ready, 1)
            dve.wait_ge(rows_stored, 16)
            v.tensor_copy(hb[:, 0:1], bm1[:, 0:1]).then_inc(setup_done, 1)
            dve.wait_ge(setup_done, 1)

            def norm(b, x_, stats, n0, st, mv, eps, rstd, rstd_ready, dst, ready):
                for t in range(NT):
                    v.bn_stats(st[:, t, :], x_[:, t, :]).then_inc(stats.sem, 1)
                dve.wait_ge(stats.sem, stats.at(b, n0 + 2))
                alone()
                for t in range(NT):
                    v.bn_aggr(mv[:, t, :], st[:, t, :]).then_inc(stats.sem, 1)
                dve.wait_ge(stats.sem, stats.at(b, n0 + 4))
                v.tensor_scalar(rstd[:, :, :], mv[:, :, 1:2], eps, None, ALU.add).then_inc(rstd_ready.sem, 1)
                dve.wait_ge(rstd_ready.sem, rstd_ready.at(b, n0 // 2 + 2))
                for t in range(NT):
                    v.tensor_scalar(dst[:, t, :], x_[:, t, :], mv[:, t, 0:1], rstd[:, t, :], ALU.subtract, ALU.mult)\
                        .then_inc(ready.sem, 1)

            def fill(slot, a):
                for name in FILL.get(slot, []) if a is not None else []:
                    if name in L0.of and name not in ("ctxT", "nxT", "sc", "PT", "lgT") and name[0] != "h":
                        dve.wait_ge(L0.sem(name), L0.at(a, name))
                    if name == "nx":
                        dve.wait_ge(x_loaded.sem, x_loaded.at(a))
                        if later(a):
                            dve.wait_ge(L0.sem("PT"), L0.at(a - 1, "PT"))
                        norm(a, x_in, stats0, 0, st0, mv0, EPS0, rstd0, rstd0_ready, nx, nx_ready)
                        if later(a):
                            dve.wait_ge(tanh0.sem, tanh0.at(a - 1))
                            dve.wait_ge(biased0.sem, biased0.at(a - 1))
                        v.tensor_copy(hb[:, :].unsqueeze(1), hid_bias[:, bass.ds(a, 1), :]).then_inc(hb_ready.sem, 1)
                    if name == "kp":
                        v.tensor_copy(kpT[:, :, :], L0.bank(name)[:, :].rearrange("p (c t) -> p c t", c=NC)).then_inc(kp_ready.sem, 1)
                    if name == "sc":
                        dve.wait_ge(L0.sem(name), L0.at(a, name))
                        v.tensor_reduce(nm0[:, :], L0.bank(name)[:, :].rearrange("p (t k) -> p t k", t=NT),
                                        axis=AX_X, op=ALU.max, negate=True).then_inc(nm0_ready.sem, 1)
                        dve.wait_ge(exp0_ready.sem, exp0_ready.at(a))
                        v.reciprocal(r0[:, :], sum0[:, :]).then_inc(r0_ready.sem, 1)
                        dve.wait_ge(r0_ready.sem, r0_ready.at(a))
                        for t in range(NT):
                            v.tensor_scalar(p0[:, t, :], p0[:, t, :], r0[:, t:t + 1], None, ALU.mult).then_inc(p0_ready.sem, 1)
                    if name == "evT":
                        v.tensor_copy(evT[:, :, :], L0.bank(name)[:, :].rearrange("p (c t) -> p c t", c=NC)).then_inc(evT_ready.sem, 1)
                    if name == "lg":
                        lg = L0.bank(name)[:, 0:4 * NT].rearrange("p (t e) -> p t e", t=NT)[:, :, 0:E]
                        v.tensor_reduce(lmax[:, :, 0], lg, axis=AX_X, op=ALU.max).then_inc(router.sem, 1)
                        dve.wait_ge(router.sem, router.at(a, 1))
                        v.tensor_tensor(lsub[:, :, :], lg, lmax[:, :, :].broadcast_to([P, NT, E]), ALU.subtract).then_inc(router.sem, 1)
                        dve.wait_ge(lexp_ready.sem, lexp_ready.at(a))
                        v.tensor_reduce(lsum[:, :, 0], lexp[:, :, :], axis=AX_X, op=ALU.add).then_inc(router.sem, 1)
                        dve.wait_ge(router.sem, router.at(a, 3))
                        v.reciprocal(lrec[:, :, :], lsum[:, :, :]).then_inc(router.sem, 1)
                        dve.wait_ge(router.sem, router.at(a, 4))
                        v.tensor_tensor(prob[:, :, :], lexp[:, :, :], lrec[:, :, :].broadcast_to([P, NT, E]), ALU.mult).then_inc(router.sem, 1)
                        dve.wait_ge(router.sem, router.at(a, 5))
                        for e in range(E):
                            if e:
                                dve.wait_ge(mix.sem, mix.at(a, 2 * e))
                            for t in range(NT):
                                v.scalar_tensor_tensor(acc[:, t, :], e_b2_all[:, e, :], prob[:, t, e:e + 1],
                                                       acc[:, t, :] if e else out_b_all[:, :], ALU.mult, ALU.add)\
                                    .then_inc(mix.sem, 1)
                    if name == "g":
                        v.tensor_tensor(zg[:, :, :], L0.bank(name)[:, :].rearrange("p (t c) -> p t c", t=NT),
                                        gate_b2_all[:, :, :].broadcast_to([P, NT, C]), ALU.add).then_inc(zg_ready.sem, 1)
                    if name[0] == "y":
                        n = int(name[1:])
                        e, t = n // NT, n % NT
                        dve.wait_ge(mix.sem, mix.at(a, 5 + n))
                        v.scalar_tensor_tensor(acc[:, t, :], L0.bank(name)[:, 0:C], prob[:, t, e:e + 1], acc[:, t, :],
                                               ALU.mult, ALU.add).then_inc(mix.sem, 1)
                        if n == E * NT - 1:
                            dve.wait_ge(mix.sem, mix.at(a))
                            dve.wait_ge(tg_ready.sem, tg_ready.at(a))
                            v.scalar_tensor_tensor(acc[:, :, :], zg[:, :, :], 1.0, acc[:, :, :], ALU.add, ALU.mult)\
                                .then_inc(x1_ready.sem, 1)
                            dve.wait_ge(x1_ready.sem, x1_ready.at(a, 1))
                            dve.wait_ge(x_copied.sem, x_copied.at(a))
                            if later(a):
                                dve.wait_ge(xb_ready.sem, xb_ready.at(a - 1, 1))
                            v.tensor_tensor(x1[:, :, :], acc[:, :, :], x_res[:, :, :], ALU.add).then_inc(x1_ready.sem, 1)

            def norm1(b, n, src):
                if n:
                    dve.wait_ge(xs_ready.sem, xs_ready.at(b, n))
                else:
                    dve.wait_ge(x1_ready.sem, x1_ready.at(b))
                    if later(b):
                        dve.wait_ge(hT_ready.sem, hT_ready.at(b - 1))
                norm(b, src, stats1, 4 * n, st1, mv1, EPS1, rstd1, rstd1_ready, xn, xn_ready)

            def values(b, name, va, ready):
                dve.wait_ge(L1.sem(name), L1.at(b, name))
                if later(b):
                    dve.wait_ge(o_ready.sem, o_ready.at(b - 1))
                for t in range(NT):
                    v.tensor_copy(va[:, t, :, 0:D], L1.bank(name)[:, t * C:(t + 1) * C].rearrange("p (h d) -> p h d", h=H))\
                        .then_inc(ready.sem, 1)

            def heads(b, name, w, n0, parts):
                sums = L1.bank((name, w))[:, 0:H * VA].rearrange("p (h d) -> p h d", h=H)
                dve.wait_ge(L1.sem((name, w)), L1.at(b, (name, w), parts))
                v.reciprocal(ro[:, w, :, :], sums[:, :, D:VA]).then_inc(ro_ready.sem, 1)
                dve.wait_ge(ro_ready.sem, ro_ready.at(b, n0 + w + 1))
                v.tensor_tensor(o[:, w, :].rearrange("p (h d) -> p h d", h=H), sums[:, :, 0:D],
                                ro[:, w, :, :].broadcast_to([P, H, D]), ALU.mult).then_inc(o_ready.sem, 1)

            def residual(b, name, s, products):
                dve.wait_ge(products.sem(name), products.at(b, name))
                src = products.bank(name)[:, :].rearrange("p (t c) -> p t c", t=NT)
                if s == 2:
                    v.tensor_tensor(tmp[:, :, :], src, grow[:, 2 * s:2 * s + 1, :].broadcast_to([P, NT, C]), ALU.mult)\
                        .then_inc(gy_ready.sem, 1)
                    dve.wait_ge(gy_ready.sem, gy_ready.at(b))
                    src = tmp[:, :, :]
                dve.wait_ge(xb_ready.sem, xb_ready.at(b, s + 1))
                if s == 0 and later(b):
                    dve.wait_ge(stored.sem, stored.at(b - 1))
                v.tensor_tensor(xs[:, :, :], src, xb[:, :, :], ALU.add).then_inc(xs_ready.sem, 1)

            def top16(b, g):
                S, r = L1.bank(("S2", g)), g % 2
                dve.wait_ge(L1.sem(("S2", g)), L1.at(b, ("S2", g)))
                alone()
                for u in range(2):
                    v.max(m8[:, r, u, :], S[:, u * T:(u + 1) * T]).then_inc(top.sem, 1)
                for u in range(2):
                    dve.wait_ge(top.sem, top.at(b, 9 * g + 1 + u))
                    alone()
                    v.match_replace(s1[:, u * T:(u + 1) * T], m8[:, r, u, :], S[:, u * T:(u + 1) * T], REPLACED)\
                        .then_inc(top.sem, 1)
                if g >= 2:
                    dve.wait_ge(rest_ready.sem, rest_ready.at(b, 2 * g - 2))
                    dve.wait_ge(p2_ready.sem, p2_ready.at(b, g - 1))
                v.tensor_scalar(nmc[:, r, :], m8[:, r, 0:2, 0], -1.0, None, ALU.mult).then_inc(top.sem, 1)
                for u in range(2):
                    dve.wait_ge(top.sem, top.at(b, 9 * g + 3 + u))
                    alone()
                    v.max(m8[:, r, 2 + u, :], s1[:, u * T:(u + 1) * T]).then_inc(top.sem, 1)
                for u in range(2):
                    dve.wait_ge(top.sem, top.at(b, 9 * g + 6 + u))
                    alone()
                    v.match_replace(s2[:, r, u * T:(u + 1) * T], m8[:, r, 2 + u, :], s1[:, u * T:(u + 1) * T], REPLACED)\
                        .then_inc(top.sem, 1)

            def gate(c, j):
                dve.wait_ge(tanh1.sem, tanh1.at(c, j + 1))
                dve.wait_ge(biased1.sem, biased1.at(c, j + 1))
                v.scalar_tensor_tensor(gated[:, j, :], thm[:, j % 4, :], 1.0, gated[:, j, :], ALU.add, ALU.mult)\
                    .then_inc(silu1.sem, 1)
                dve.wait_ge(LM.sem(("m", j)), LM.at(c, ("m", j)))
                dve.wait_ge(silu1.sem, silu1.at(c, j + 1))
                v.scalar_tensor_tensor(gated[:, j, :], LM.bank(("m", j))[:, T:2 * T], bm1[:, HID // P + j:HID // P + j + 1],
                                       gated[:, j, :], ALU.add, ALU.mult).then_inc(gated_ready.sem, 1)

            def iteration(a, b, c):
                if b is not None:
                    dve.wait_ge(ones_ready, 2)
                    values(b, "v2", va2, va2_ready)
                fill("norm3", a)
                for j in range(HID // P):
                    if c is not None:
                        gate(c, j)
                    fill(("mlp", j), a)
                    if j == NORM1_STEP and b is not None:
                        norm1(b, 0, x1)
                        v.tensor_copy(ad[:, :].unsqueeze(1), ada[:, bass.ds(b, 1), :]).then_inc(ad_ready.sem, 1)
                fill("silu", a)
                if c is not None:
                    residual(c, "y", 2, LM)
                fill("proj1", a)
                if b is not None:
                    dve.wait_ge(L1.sem("k1"), L1.at(b, "k1"))
                    for t in range(NC):
                        v.tensor_scalar(kT1[:, t, :], L1.bank("k1")[:, t * T:(t + 1) * T], bk1[:, t:t + 1], None, ALU.add)\
                            .then_inc(k1_ready.sem, 1)
                    dve.wait_ge(k1_ready.sem, k1_ready.at(b))
                    for h in range(HPT):
                        v.tensor_scalar(KM[:, h, :], kT1[:, 0, :], head_mask[:, h:h + 1], None, ALU.mult)\
                            .then_inc(km1a_ready.sem, 1)
                    values(b, "v1", va1, va1_ready)
                fill("keys1", a)
                for s in range(SELF_GROUPS + PV_LAG):
                    if b is not None and s < SELF_GROUPS:
                        dve.wait_ge(L1.sem(("S1", s)), L1.at(b, ("S1", s)))
                        v.tensor_reduce(nms[:, s % 2, :], L1.bank(("S1", s))[:, :].rearrange("p (h k) -> p h k", h=4),
                                        axis=AX_X, op=ALU.max, negate=True).then_inc(max1_ready.sem, 1)
                    fill(("self", s), a)
                    if b is not None and s == 4 + PV_LAG:
                        heads(b, "O1", 0, 0, 4)
                if b is not None:
                    heads(b, "O1", 1, 0, 4)
                fill("heads1", a)
                fill("out1", a)
                if b is not None:
                    residual(b, "so", 0, L1)
                    norm1(b, 1, xs)
                fill("norm2", a)
                fill("proj2", a)
                fill("keys2", a)
                for s in range(CROSS_GROUPS + PV_LAG):
                    if b is not None and s < CROSS_GROUPS:
                        top16(b, s)
                    fill(("cross", s), a)
                    if b is not None and s == 8 + PV_LAG:
                        heads(b, "O2", 0, 2, 8)
                if b is not None:
                    heads(b, "O2", 1, 2, 8)
                fill("heads2", a)
                fill("out2", a)
                if b is not None:
                    residual(b, "co", 1, L1)
                    norm1(b, 2, xs)
                fill("end", a)

            iteration(0, None, None)
            iteration(1, 0, None)
            with dve.Fori(2, B) as i:
                iteration(i, i - 1, i - 2)
            iteration(None, B - 1, B - 2)
            iteration(None, None, B - 1)

        @block.tensor
        def _(pe):
            def mm(out_, lhsT, rhs, k, n):
                return nc.tensor.matmul(out_, lhsT, rhs, start=(k == 0), stop=(k == n - 1))

            pe.wait_ge(ident_ready, 1)
            pe.wait_ge(square_loaded, SQUARE_LOADED)
            for i, p in enumerate(SETUP):
                bank, kind = banks[i % 8], p[0]
                if i >= 8:
                    pe.wait_ge(setup_ev, i - 7)
                if p == ("tw2", 0):
                    pe.wait_ge(w2_loaded, W2_LOADED)
                if p == ("wqk", 0):
                    pe.wait_ge(setup_ev, SETUP.index(("tv", NC - 1)) + 1)
                if p == ("w2", 0):
                    pe.wait_ge(setup_ev, SETUP.index(("tw2", 5)) + 1)
                if p == ("ev", 0, 0):
                    pe.wait_ge(evidence_loaded, EVIDENCE_LOADED)
                if p == ("eb2", 0):
                    pe.wait_ge(anchor_loaded, ANCHOR_LOADED)
                    pe.wait_ge(scond_ready, 4)
                if p == ("ada",):
                    pe.wait_ge(ada_loaded, ADA_LOADED)
                if kind in ("tq", "tk", "tv"):
                    src = {"tq": raw_q, "tk": raw_k, "tv": raw_v}[kind]
                    for c in range(NC):
                        last = nc.tensor.transpose(bank[:, c * P:(c + 1) * P], src[:, c, p[1] * P:(p[1] + 1) * P], ident[:, :])
                elif kind == "tw2":
                    for k in range(2):
                        for c in range(NC):
                            last = nc.tensor.transpose(bank[:, c * 2 * P + k * P:c * 2 * P + (k + 1) * P],
                                                       w2[:, 2 * p[1] + k, c * P:(c + 1) * P], ident[:, :])
                elif kind == "wqk":
                    for k in range(NC):
                        last = mm(bank[:, 0:C], tk[:, k, p[1] * P:(p[1] + 1) * P], tq[:, k, :], k, NC)
                elif kind == "ev":
                    n = min(512, W1_COLS - p[2])
                    for k in range(NC):
                        last = mm(bank[:, 0:n], tv[:, k, p[1] * P:(p[1] + 1) * P], raw_ev[:, k, p[2]:p[2] + n], k, NC)
                elif kind == "w2":
                    for u in range(2):
                        for k in range(NC):
                            f = (2 * p[1] + u) * P
                            last = mm(bank[:, u * C:(u + 1) * C], tw2[:, k, f:f + P], raw_o[:, k, :], k, NC)
                elif kind == "eb2":
                    for k in range(NC):
                        last = mm(bank[:, 0:C], eb2_cols[:, k, p[1], :], raw_o[:, k, :], k, NC)
                elif kind == "hid":
                    for j in range(NCH):
                        for k in range(NC):
                            last = mm(bank[:, j * B:(j + 1) * B], raw_an[:, k, j * P:(j + 1) * P], cond_col[:, k, :], k, NC)
                elif kind == "rout":
                    for k in range(NC):
                        last = mm(bank[0:E, 0:B], raw_an[:, k, ROUT_COL:W1_COLS], cond_col[:, k, :], k, NC)
                elif kind == "ada":
                    for j in range(6 * NC):
                        n, u = j // 4, j % 4
                        for k in range(NC):
                            lo = 3 * n * C + u * P
                            last = mm(bank[:, j * B:(j + 1) * B], raw_ada[:, k, lo:lo + P], scond[:, k, :], k, NC)
                elif kind == "gate":
                    for k in range(NC):
                        lo = (3 * p[1] + 2) * C
                        last = mm(bank[0:B, 0:C], scond[:, k, :], raw_ada[:, k, lo:lo + C], k, NC)
                elif kind == "bias":
                    if p[1] == 0:
                        pe.wait_ge(weights_loaded, WEIGHTS_LOADED)
                    for k in range(NC):
                        last = mm(bank[0:B, 0:C], bv_cols[:, k, p[1], :], (wso, wco)[p[1]][:, k, :], k, NC)
                last.then_inc(setup_mm, 1)
            pe.wait_ge(setup_done, 1)

            def transpose4(bank, src):
                for c in range(2):
                    for t in range(2):
                        last = nc.tensor.transpose(bank[:, c * T + t * P:c * T + (t + 1) * P],
                                                   src[:, t, c * P:(c + 1) * P], ident[:, :])
                return last

            def by_channel(bank, w, lo, actT, n=NC):
                for c in range(2):
                    for k in range(n):
                        last = mm(bank[:, c * T:(c + 1) * T], w[:, k, lo + c * P:lo + (c + 1) * P], actT[:, k, :], k, n)
                return last

            def by_token(bank, actT, w, lo, n=NC):
                for t in range(NT):
                    for k in range(n):
                        last = mm(bank[:, t * C:(t + 1) * C], actT[:, k, t * P:(t + 1) * P], w[:, k, lo:lo + C], k, n)
                return last

            def comb(k):
                return nxT[:, k, :] if k < NC else evT[:, k - NC, :]

            def fill(slot, a):
                for name in FILL.get(slot, []) if a is not None else []:
                    if name == "nx":
                        continue
                    bank = L0.bank(name)
                    if name == "ctxT":
                        if later(a):
                            pe.wait_ge(mix.sem, mix.at(a - 1))
                        pe.wait_ge(ctx_loaded.sem, ctx_loaded.at(a))
                        alone()
                        last = transpose4(bank, ctx_in)
                    if name == "nxT":
                        pe.wait_ge(nx_ready.sem, nx_ready.at(a))
                        last = transpose4(bank, nx)
                    if name == "kp":
                        pe.wait_ge(ctxT_ready.sem, ctxT_ready.at(a))
                        last = by_channel(bank, wqk, 0, ctxT)
                    if name == "sc":
                        pe.wait_ge(nxT_ready.sem, nxT_ready.at(a))
                        pe.wait_ge(kp_ready.sem, kp_ready.at(a))
                        last = by_token(bank, nxT, kpT, 0)
                    if name == "PT":
                        pe.wait_ge(p0_ready.sem, p0_ready.at(a))
                        last = transpose4(bank, p0)
                    if name == "evT":
                        pe.wait_ge(exp0_ready.sem, exp0_ready.at(a))
                        pe.wait_ge(pT0_ready.sem, pT0_ready.at(a))
                        last = by_channel(bank, ctx_in, 0, pT0)
                    if name == "lgT":
                        pe.wait_ge(evT_ready.sem, evT_ready.at(a))
                        for k in range(2 * NC):
                            last = mm(bank[0:E, 0:T], w1[:, k, ROUT_COL:W1_COLS], comb(k), k, 2 * NC)
                    if name == "lg":
                        pe.wait_ge(lgT_ready.sem, lgT_ready.at(a))
                        alone()
                        for t in range(NT):
                            last = nc.tensor.transpose(bank[:, 4 * t:4 * t + E], lgT[:, t * P:(t + 1) * P], ident[0:E, 0:E])
                    if name[0] == "h":
                        n = int(name[1:])
                        if n == 1:
                            pe.wait_ge(router.sem, router.at(a, 2))
                        if n >= 2:
                            pe.wait_ge(biased0.sem, biased0.at(a, n - 1))
                        for k in range(2 * NC):
                            last = mm(bank[:, 0:T], w1[:, k, n * P:(n + 1) * P], comb(k), k, 2 * NC)
                    if name == "g":
                        pe.wait_ge(hid_ready.sem, hid_ready.at(a))
                        for t in range(NT):
                            for k in range(NC):
                                last = mm(bank[:, t * C:(t + 1) * C], hid[:, EXP_COLS // P + k, t * P:(t + 1) * P], wg2[:, k, :], k, NC)
                    if name[0] == "y":
                        n = int(name[1:])
                        e, t = n // NT, n % NT
                        if n == 1:
                            pe.wait_ge(zg_ready.sem, zg_ready.at(a))
                        if n >= 2:
                            pe.wait_ge(mix.sem, mix.at(a, 5 + n))
                        for k in range(RH // P):
                            f = e * (RH // P) + k
                            last = mm(bank[:, 0:C], hid[:, f, t * P:(t + 1) * P], w2[:, f, :], k, RH // P)
                    last.then_inc(L0.sem(name), 1)

            def alone():
                pe.nop(nofuse=True)

            def self_scores(b, g):
                w, q = g // 4, g % 4
                if g == 0:
                    pe.wait_ge(q_ready.sem, q_ready.at(b, 2))
                if g >= 2:
                    pe.wait_ge(exp1_ready.sem, exp1_ready.at(b, 4 * g - 4))
                if g < 2:
                    pe.wait_ge(km1a_ready.sem, km1a_ready.at(b, 4 * q + 4))
                elif g < 4:
                    pe.wait_ge(km1b_ready.sem, km1b_ready.at(b, 2 * q - 2))
                mm(L1.bank(("S1", g))[:, :].rearrange("p (h k) -> p h k", h=4), qT[:, q // 2, w * P:(w + 1) * P],
                   KM[:, 4 * q:4 * q + 4, w * P:(w + 1) * P], 0, 1).then_inc(L1.sem(("S1", g)), 1)

            def self_transposes(b, g):
                if g == 1:
                    pe.wait_ge(va1_ready.sem, va1_ready.at(b))
                if g >= 2:
                    pe.wait_ge(et1_ready.sem, et1_ready.at(b, g - 1))
                pe.wait_ge(exp1_ready.sem, exp1_ready.at(b, 4 * g + 4))
                for u in range(4):
                    last = nc.tensor.transpose(L1.bank(("T1", g))[:, u * P:(u + 1) * P], es[:, g % 3, u * P:(u + 1) * P], ident[:, :])
                last.then_inc(L1.sem(("T1", g)), 1)

            def self_pv(b, g):
                w, q = g // 4, g % 4
                if g == 0 and later(b):
                    pe.wait_ge(gy_ready.sem, gy_ready.at(b - 1))
                if g == 4 and later(b):
                    pe.wait_ge(o_ready.sem, o_ready.at(b - 1))
                pe.wait_ge(et1_ready.sem, et1_ready.at(b, g + 1))
                if g == 0:
                    pe.wait_ge(va1_ready.sem, va1_ready.at(b))
                for u in range(4):
                    h = 4 * q + u
                    last = mm(L1.bank(("O1", w))[:, h * VA:(h + 1) * VA], et[:, g % 2, u * P:(u + 1) * P], va1[:, w, h, :], 0, 1)
                last.then_inc(L1.sem(("O1", w)), 1)

            def cross_scores(b, g):
                t, p = g // 8, g % 8
                if g == 0:
                    pe.wait_ge(q_ready.sem, q_ready.at(b, 4))
                if g >= 2:
                    pe.wait_ge(exp2_ready.sem, exp2_ready.at(b, 2 * g - 2))
                if g < 8:
                    pe.wait_ge(km2_ready.sem, km2_ready.at(b, p + 1))
                mm(L1.bank(("S2", g))[:, :].rearrange("p (h k) -> p h k", h=2), qT[:, p // 4, t * P:(t + 1) * P],
                   KM[:, 2 * p:2 * p + 2, :], 0, 1).then_inc(L1.sem(("S2", g)), 1)

            def cross_transposes(b, g):
                if g >= 2:
                    pe.wait_ge(et2_ready.sem, et2_ready.at(b, g - 1))
                pe.wait_ge(p2_ready.sem, p2_ready.at(b, g + 1))
                for u in range(4):
                    last = nc.tensor.transpose(L1.bank(("T2", g))[:, u * P:(u + 1) * P], es[:, g % 3, u * P:(u + 1) * P], ident[:, :])
                last.then_inc(L1.sem(("T2", g)), 1)

            def cross_pv(b, g):
                t, p = g // 8, g % 8
                pe.wait_ge(et2_ready.sem, et2_ready.at(b, g + 1))
                if g == 0:
                    pe.wait_ge(va2_ready.sem, va2_ready.at(b))
                for u in range(2):
                    h = 2 * p + u
                    for k in range(NT):
                        last = mm(L1.bank(("O2", t))[:, h * VA:(h + 1) * VA], et[:, g % 2, (2 * u + k) * P:(2 * u + k + 1) * P],
                                  va2[:, k, h, :], k, NT)
                last.then_inc(L1.sem(("O2", t)), 1)

            def attention(a, b, kind, groups, scores, transposes, pv):
                for s in range(groups + PV_LAG):
                    if b is not None and s < groups:
                        scores(b, s)
                    fill((kind, s), a)
                    if b is not None and 0 <= s - S_LAG < groups:
                        transposes(b, s - S_LAG)
                    if b is not None and 0 <= s - PV_LAG < groups:
                        pv(b, s - PV_LAG)

            def iteration(a, b, c):
                if c is not None:
                    pe.wait_ge(xn_ready.sem, xn_ready.at(c, 6))
                    transpose4(LM.bank("hT3"), xn).then_inc(LM.sem("hT3"), 1)
                if b is not None:
                    pe.wait_ge(ctxT_ready.sem, ctxT_ready.at(b))
                    by_channel(L1.bank("k2"), wkv, 0, ctxT).then_inc(L1.sem("k2"), 1)
                    by_token(L1.bank("v2"), ctxT, wkv, C).then_inc(L1.sem("v2"), 1)
                fill("norm3", a)
                for j in range(HID // P):
                    if c is not None:
                        if j == 0:
                            pe.wait_ge(hT_ready.sem, hT_ready.at(c, 6))
                            if b is not None:
                                pe.wait_ge(k2_ready.sem, k2_ready.at(b))
                        if j == 1 and b is not None:
                            pe.wait_ge(va2_ready.sem, va2_ready.at(b))
                        if j == 2:
                            pe.wait_ge(xs_ready.sem, xs_ready.at(c, 2))
                        if j >= 4:
                            pe.wait_ge(gated_ready.sem, gated_ready.at(c, j - 3))
                        for u in range(2):
                            for k in range(NC):
                                lo = u * HID + j * P
                                last = mm(LM.bank(("m", j))[:, u * T:(u + 1) * T], wm1[:, k, lo:lo + P], hT[:, k, :], k, NC)
                        last.then_inc(LM.sem(("m", j)), 1)
                    fill(("mlp", j), a)
                if b is not None:
                    pe.wait_ge(xn_ready.sem, xn_ready.at(b, 2))
                    transpose4(L1.bank("hT1"), xn).then_inc(L1.sem("hT1"), 1)
                fill("silu", a)
                if c is not None:
                    pe.wait_ge(gated_ready.sem, gated_ready.at(c))
                    by_token(LM.bank("y"), gated, wm2, 0, HID // P).then_inc(LM.sem("y"), 1)
                fill("proj1", a)
                if b is not None:
                    pe.wait_ge(hT_ready.sem, hT_ready.at(b, 2))
                    by_channel(L1.bank("q1"), wqkv, 0, hT).then_inc(L1.sem("q1"), 1)
                    by_channel(L1.bank("k1"), wqkv, C, hT).then_inc(L1.sem("k1"), 1)
                    by_token(L1.bank("v1"), hT, wqkv, 2 * C).then_inc(L1.sem("v1"), 1)
                fill("keys1", a)
                attention(a, b, "self", SELF_GROUPS, self_scores, self_transposes, self_pv)
                fill("heads1", a)
                if b is not None:
                    pe.wait_ge(o_ready.sem, o_ready.at(b, 2))
                    transpose4(L1.bank("oT1"), o).then_inc(L1.sem("oT1"), 1)
                fill("out1", a)
                if b is not None:
                    pe.wait_ge(oT_ready.sem, oT_ready.at(b, 1))
                    pe.wait_ge(wgated_ready.sem, wgated_ready.at(b, 1))
                    by_token(L1.bank("so"), oT, wso_gated, 0).then_inc(L1.sem("so"), 1)
                fill("norm2", a)
                if b is not None:
                    pe.wait_ge(xn_ready.sem, xn_ready.at(b, 4))
                    transpose4(L1.bank("hT2"), xn).then_inc(L1.sem("hT2"), 1)
                fill("proj2", a)
                if b is not None:
                    pe.wait_ge(hT_ready.sem, hT_ready.at(b, 4))
                    pe.wait_ge(xs_ready.sem, xs_ready.at(b, 1))
                    by_channel(L1.bank("q2"), wq2, 0, hT).then_inc(L1.sem("q2"), 1)
                fill("keys2", a)
                attention(a, b, "cross", CROSS_GROUPS, cross_scores, cross_transposes, cross_pv)
                fill("heads2", a)
                if b is not None:
                    pe.wait_ge(o_ready.sem, o_ready.at(b, 4))
                    transpose4(L1.bank("oT2"), o).then_inc(L1.sem("oT2"), 1)
                fill("out2", a)
                if b is not None:
                    pe.wait_ge(oT_ready.sem, oT_ready.at(b, 2))
                    pe.wait_ge(wgated_ready.sem, wgated_ready.at(b, 2))
                    by_token(L1.bank("co"), oT, wco_gated, 0).then_inc(L1.sem("co"), 1)
                fill("end", a)

            iteration(0, None, None)
            iteration(1, 0, None)
            with pe.Fori(2, B) as i:
                iteration(i, i - 1, i - 2)
            iteration(None, B - 1, B - 2)
            iteration(None, None, B - 1)

    return nc


_L0 = ["ln_gamma", "ln_beta", "Wq", "Wk", "Wv", "router_W", "router_b", "e_w1", "e_b1", "e_w2", "e_b2",
       "gate_w1", "gate_b1", "gate_w2", "gate_b2", "out_w", "out_b"]
_L1 = ["w_ada", "b_ada", "w_qkv", "b_qkv", "w_so", "b_so", "w_q", "b_q", "w_kv", "b_kv", "w_co", "b_co",
       "w_m1", "b_m1", "w_m2", "b_m2"]
_INS = ["x", "cond_1024", "ctx_1024"] + ["L0_xcond_" + n for n in _L0] + ["L1_xcond_" + n for n in _L1]


def kernel(**inputs):
    import numpy as _np
    import concourse.bacc as _bacc
    from concourse.bass_utils import run_bass_kernel_spmd as _run

    nc = _bacc.Bacc("TRN2", target_bir_lowering=False, num_devices=1)
    arrays, args = {}, []
    for name in _INS:
        a = _np.ascontiguousarray(inputs[name])
        arrays[f"in_{name}_dram"] = a
        args.append(nc.dram_tensor(f"in_{name}_dram", a.shape, mybir.dt.from_np(a.dtype), kind="ExternalInput").ap())
    args.append(nc.dram_tensor("out_dram", (B, T, C), F32, kind="ExternalOutput").ap())
    build(nc, *args)
    r = _run(nc, [arrays], core_ids=[0])
    return r.results[0]["out_dram"]
```
